# Optimizing a Trainium2 kernel written in Bass

```python
import numpy as np
import jax
import jax.numpy as jnp

def _softmax(x, axis=-1):
    return jax.nn.softmax(x, axis=axis)

def _gelu(x):
    return jax.nn.gelu(x, approximate=True)

def _silu(x):
    return jax.nn.silu(x)

def _sigmoid(x):
    return jax.nn.sigmoid(x)

def _layernorm(x, axis=-1, eps=1e-05):
    m = jnp.mean(x, axis=axis, keepdims=True)
    v = jnp.var(x, axis=axis, keepdims=True)
    return (x - m) / jnp.sqrt(v + eps)

def _scatter_add(tgt, idx, src, axis=0):
    return tgt.at[idx].add(src)

def _segment_sum(src, seg, n):
    return jax.ops.segment_sum(src, seg, n)
kernel_name = 'mk_dlrm_tower_d1_rec_r8_eac613'

def setup_inputs(seed: int=0):
    np.random.seed(seed)
    _w = jnp.asarray

    def _rec_inputs():
        import jax
        import jax.numpy as jnp
        _tk = jax.random.key(seed)
        dense_ctx = jax.random.normal(jax.random.fold_in(_tk, 190), (512, 16), jnp.float32)
        ids = jnp.stack([jax.random.randint(jax.random.fold_in(_tk, 200 + f), (512,), 0, v, jnp.int32) for f, v in enumerate([1000, 1000, 1000, 1250, 12500, 1000, 1250, 125000, 12500, 1250, 1250, 1250, 1250, 12500, 1000, 125000, 125000, 1250, 1000, 1250, 12500, 12500, 12500, 1250, 1250, 1000, 12500, 1250, 1250, 1000, 1250, 1250])], axis=1)
        tbl_0 = 0.05 * jax.random.normal(jax.random.fold_in(_tk, 500 + 0), (1000, 64), jnp.float32)
        tbl_1 = 0.05 * jax.random.normal(jax.random.fold_in(_tk, 500 + 1), (1000, 64), jnp.float32)
        tbl_2 = 0.05 * jax.random.normal(jax.random.fold_in(_tk, 500 + 2), (1000, 64), jnp.float32)
        tbl_3 = 0.05 * jax.random.normal(jax.random.fold_in(_tk, 500 + 3), (1250, 64), jnp.float32)
        tbl_4 = 0.05 * jax.random.normal(jax.random.fold_in(_tk, 500 + 4), (12500, 64), jnp.float32)
        tbl_5 = 0.05 * jax.random.normal(jax.random.fold_in(_tk, 500 + 5), (1000, 64), jnp.float32)
        tbl_6 = 0.05 * jax.random.normal(jax.random.fold_in(_tk, 500 + 6), (1250, 64), jnp.float32)
        tbl_7 = 0.05 * jax.random.normal(jax.random.fold_in(_tk, 500 + 7), (125000, 64), jnp.float32)
        tbl_8 = 0.05 * jax.random.normal(jax.random.fold_in(_tk, 500 + 8), (12500, 64), jnp.float32)
        tbl_9 = 0.05 * jax.random.normal(jax.random.fold_in(_tk, 500 + 9), (1250, 64), jnp.float32)
        tbl_10 = 0.05 * jax.random.normal(jax.random.fold_in(_tk, 500 + 10), (1250, 64), jnp.float32)
        tbl_11 = 0.05 * jax.random.normal(jax.random.fold_in(_tk, 500 + 11), (1250, 64), jnp.float32)
        tbl_12 = 0.05 * jax.random.normal(jax.random.fold_in(_tk, 500 + 12), (1250, 64), jnp.float32)
        tbl_13 = 0.05 * jax.random.normal(jax.random.fold_in(_tk, 500 + 13), (12500, 64), jnp.float32)
        tbl_14 = 0.05 * jax.random.normal(jax.random.fold_in(_tk, 500 + 14), (1000, 64), jnp.float32)
        tbl_15 = 0.05 * jax.random.normal(jax.random.fold_in(_tk, 500 + 15), (125000, 64), jnp.float32)
        tbl_16 = 0.05 * jax.random.normal(jax.random.fold_in(_tk, 500 + 16), (125000, 64), jnp.float32)
        tbl_17 = 0.05 * jax.random.normal(jax.random.fold_in(_tk, 500 + 17), (1250, 64), jnp.float32)
        tbl_18 = 0.05 * jax.random.normal(jax.random.fold_in(_tk, 500 + 18), (1000, 64), jnp.float32)
        tbl_19 = 0.05 * jax.random.normal(jax.random.fold_in(_tk, 500 + 19), (1250, 64), jnp.float32)
        tbl_20 = 0.05 * jax.random.normal(jax.random.fold_in(_tk, 500 + 20), (12500, 64), jnp.float32)
        tbl_21 = 0.05 * jax.random.normal(jax.random.fold_in(_tk, 500 + 21), (12500, 64), jnp.float32)
        tbl_22 = 0.05 * jax.random.normal(jax.random.fold_in(_tk, 500 + 22), (12500, 64), jnp.float32)
        tbl_23 = 0.05 * jax.random.normal(jax.random.fold_in(_tk, 500 + 23), (1250, 64), jnp.float32)
        tbl_24 = 0.05 * jax.random.normal(jax.random.fold_in(_tk, 500 + 24), (1250, 64), jnp.float32)
        tbl_25 = 0.05 * jax.random.normal(jax.random.fold_in(_tk, 500 + 25), (1000, 64), jnp.float32)
        tbl_26 = 0.05 * jax.random.normal(jax.random.fold_in(_tk, 500 + 26), (12500, 64), jnp.float32)
        tbl_27 = 0.05 * jax.random.normal(jax.random.fold_in(_tk, 500 + 27), (1250, 64), jnp.float32)
        tbl_28 = 0.05 * jax.random.normal(jax.random.fold_in(_tk, 500 + 28), (1250, 64), jnp.float32)
        tbl_29 = 0.05 * jax.random.normal(jax.random.fold_in(_tk, 500 + 29), (1000, 64), jnp.float32)
        tbl_30 = 0.05 * jax.random.normal(jax.random.fold_in(_tk, 500 + 30), (1250, 64), jnp.float32)
        tbl_31 = 0.05 * jax.random.normal(jax.random.fold_in(_tk, 500 + 31), (1250, 64), jnp.float32)
        _rk = jax.random.fold_in(_tk, 7)
        W_top1 = 0.0606339 * jax.random.normal(jax.random.fold_in(_tk, 801), (272, 512), jnp.float32)
        W_top2 = 0.0441942 * jax.random.normal(jax.random.fold_in(_tk, 802), (512, 256), jnp.float32)
        W_top3 = 0.0625 * jax.random.normal(jax.random.fold_in(_tk, 803), (256, 1), jnp.float32)
        b_top1 = jnp.zeros((512,), jnp.float32)
        b_top2 = jnp.zeros((256,), jnp.float32)
        return (dense_ctx, ids, tbl_0, tbl_1, tbl_2, tbl_3, tbl_4, tbl_5, tbl_6, tbl_7, tbl_8, tbl_9, tbl_10, tbl_11, tbl_12, tbl_13, tbl_14, tbl_15, tbl_16, tbl_17, tbl_18, tbl_19, tbl_20, tbl_21, tbl_22, tbl_23, tbl_24, tbl_25, tbl_26, tbl_27, tbl_28, tbl_29, tbl_30, tbl_31, W_top1, b_top1, W_top2, b_top2, W_top3)
    dense_ctx, ids, tbl_0, tbl_1, tbl_2, tbl_3, tbl_4, tbl_5, tbl_6, tbl_7, tbl_8, tbl_9, tbl_10, tbl_11, tbl_12, tbl_13, tbl_14, tbl_15, tbl_16, tbl_17, tbl_18, tbl_19, tbl_20, tbl_21, tbl_22, tbl_23, tbl_24, tbl_25, tbl_26, tbl_27, tbl_28, tbl_29, tbl_30, tbl_31, W_top1, b_top1, W_top2, b_top2, W_top3 = _rec_inputs()

    def _L0_rec_setup():
        import jax, jax.numpy as jnp
        import numpy as np
        EMB_DIM = 64
        NUM_FIELDS = 32
        NUM_PAIRS = NUM_FIELDS * (NUM_FIELDS - 1) // 2
        D1 = 256
        BATCH = 256
        key = jax.random.key(seed)
        k1, k2, k3 = jax.random.split(key, 3)
        feat_emb = jax.random.normal(k1, (BATCH, NUM_FIELDS, EMB_DIM), dtype=jnp.float32)
        lim_k = float(np.sqrt(6.0 / (EMB_DIM + EMB_DIM)))
        kernel = jax.random.uniform(k2, (EMB_DIM, NUM_PAIRS, EMB_DIM), minval=-lim_k, maxval=lim_k, dtype=jnp.float32)
        lim_w = float(np.sqrt(6.0 / (NUM_PAIRS + D1)))
        W = jax.random.uniform(k3, (D1, NUM_PAIRS), minval=-lim_w, maxval=lim_w, dtype=jnp.float32)
        b = jnp.zeros((D1,), dtype=jnp.float32)
        return {'feat_emb': feat_emb, 'kernel': kernel, 'W': W, 'b': b}
    _L0_rec_all = _L0_rec_setup()
    _L0_rec_in = {k: v for k, v in _L0_rec_all.items() if k in ('kernel', 'W', 'b')}
    del _L0_rec_all
    return {'dense_ctx': dense_ctx, 'ids': ids, 'tbl_0': tbl_0, 'tbl_1': tbl_1, 'tbl_2': tbl_2, 'tbl_3': tbl_3, 'tbl_4': tbl_4, 'tbl_5': tbl_5, 'tbl_6': tbl_6, 'tbl_7': tbl_7, 'tbl_8': tbl_8, 'tbl_9': tbl_9, 'tbl_10': tbl_10, 'tbl_11': tbl_11, 'tbl_12': tbl_12, 'tbl_13': tbl_13, 'tbl_14': tbl_14, 'tbl_15': tbl_15, 'tbl_16': tbl_16, 'tbl_17': tbl_17, 'tbl_18': tbl_18, 'tbl_19': tbl_19, 'tbl_20': tbl_20, 'tbl_21': tbl_21, 'tbl_22': tbl_22, 'tbl_23': tbl_23, 'tbl_24': tbl_24, 'tbl_25': tbl_25, 'tbl_26': tbl_26, 'tbl_27': tbl_27, 'tbl_28': tbl_28, 'tbl_29': tbl_29, 'tbl_30': tbl_30, 'tbl_31': tbl_31, 'W_top1': W_top1, 'b_top1': b_top1, 'W_top2': W_top2, 'b_top2': b_top2, 'W_top3': W_top3, 'L0_rec_kernel': _L0_rec_in['kernel'], 'L0_rec_W': _L0_rec_in['W'], 'L0_rec_b': _L0_rec_in['b']}

def reference(dense_ctx, ids, tbl_0, tbl_1, tbl_2, tbl_3, tbl_4, tbl_5, tbl_6, tbl_7, tbl_8, tbl_9, tbl_10, tbl_11, tbl_12, tbl_13, tbl_14, tbl_15, tbl_16, tbl_17, tbl_18, tbl_19, tbl_20, tbl_21, tbl_22, tbl_23, tbl_24, tbl_25, tbl_26, tbl_27, tbl_28, tbl_29, tbl_30, tbl_31, W_top1, b_top1, W_top2, b_top2, W_top3, L0_rec_kernel, L0_rec_W, L0_rec_b):
    import jax
    import jax.numpy as jnp

    def _L0_rec_ref(feat_emb, kernel, W, b):
        import jax, jax.numpy as jnp
        import numpy as np
        EMB_DIM = 64
        NUM_FIELDS = 32
        NUM_PAIRS = NUM_FIELDS * (NUM_FIELDS - 1) // 2
        D1 = 256
        BATCH = 256
        num_fields = feat_emb.shape[1]
        rows, cols = np.triu_indices(num_fields, k=1)
        p = feat_emb[:, rows, :]
        q = feat_emb[:, cols, :]
        pij = jnp.einsum('bpe,dpe,bpd->bp', p, kernel, q)
        return pij @ W.T + b
    e = jnp.stack([tbl_0[ids[:, 0]], tbl_1[ids[:, 1]], tbl_2[ids[:, 2]], tbl_3[ids[:, 3]], tbl_4[ids[:, 4]], tbl_5[ids[:, 5]], tbl_6[ids[:, 6]], tbl_7[ids[:, 7]], tbl_8[ids[:, 8]], tbl_9[ids[:, 9]], tbl_10[ids[:, 10]], tbl_11[ids[:, 11]], tbl_12[ids[:, 12]], tbl_13[ids[:, 13]], tbl_14[ids[:, 14]], tbl_15[ids[:, 15]], tbl_16[ids[:, 16]], tbl_17[ids[:, 17]], tbl_18[ids[:, 18]], tbl_19[ids[:, 19]], tbl_20[ids[:, 20]], tbl_21[ids[:, 21]], tbl_22[ids[:, 22]], tbl_23[ids[:, 23]], tbl_24[ids[:, 24]], tbl_25[ids[:, 25]], tbl_26[ids[:, 26]], tbl_27[ids[:, 27]], tbl_28[ids[:, 28]], tbl_29[ids[:, 29]], tbl_30[ids[:, 30]], tbl_31[ids[:, 31]]], axis=1)
    z = _L0_rec_ref(e, L0_rec_kernel, L0_rec_W, L0_rec_b)
    z = z.reshape(z.shape[0], -1)
    h = jnp.concatenate([z, dense_ctx], axis=1)
    h = jnp.maximum(h @ W_top1 + b_top1, 0.0)
    h = jnp.maximum(h @ W_top2 + b_top2, 0.0)
    y = h @ W_top3
    return y

_drawn_inputs = setup_inputs


def setup_inputs(seed=0):
    import zlib

    import numpy as np

    out = dict(_drawn_inputs(seed))
    spreads = {'b_top1': (0.0, 0.1), 'b_top2': (0.0, 0.1), 'L0_rec_b': (0.0, 0.1)}
    factors = {'tbl_0': 3.37,
     'tbl_1': 3.376,
     'tbl_2': 3.261,
     'tbl_3': 3.295,
     'tbl_4': 3.389,
     'tbl_5': 3.449,
     'tbl_6': 3.074,
     'tbl_7': 3.337,
     'tbl_8': 3.372,
     'tbl_9': 3.153,
     'tbl_10': 3.337,
     'tbl_11': 3.409,
     'tbl_12': 3.138,
     'tbl_13': 3.322,
     'tbl_14': 3.433,
     'tbl_15': 3.421,
     'tbl_16': 3.602,
     'tbl_17': 3.23,
     'tbl_18': 3.199,
     'tbl_19': 2.995,
     'tbl_20': 3.051,
     'tbl_21': 3.463,
     'tbl_22': 3.704,
     'tbl_23': 2.921,
     'tbl_24': 3.386,
     'tbl_25': 3.027,
     'tbl_26': 3.465,
     'tbl_27': 3.439,
     'tbl_28': 3.572,
     'tbl_29': 3.501,
     'tbl_30': 3.194,
     'tbl_31': 3.471}
    for name, (base, spread) in spreads.items():
        noise = np.random.default_rng([zlib.crc32(name.encode()), seed]).standard_normal(out[name].shape)
        drawn = base * np.exp(spread * noise) if base else spread * noise
        out[name] = jnp.asarray(drawn.astype(out[name].dtype))
    for name, factor in factors.items():
        out[name] = (out[name] * factor).astype(out[name].dtype)
    return out
```

```python
from contextlib import ExitStack

import numpy as np

import concourse.bass as bass
from concourse import mybir

F32 = mybir.dt.float32
F32R = mybir.dt.float32r
I32 = mybir.dt.int32
U32 = mybir.dt.uint32
ALU = mybir.AluOpType
ACT = mybir.ActivationFunctionType

P = 128
BATCH = 512
BT = BATCH // P
FIELDS = 32
D = 64
COUPLES = FIELDS // 2
PAIRS = FIELDS * (FIELDS - 1) // 2
D1 = 256
DENSE = 16
H1 = 512
H2 = 256
GROUPS = COUPLES * (COUPLES - 1) // 2
GROUP_COLS = 4 * D
CHUNK_GROUPS = 8
CHUNK_COLS = CHUNK_GROUPS * GROUP_COLS
HALF_COLS = CHUNK_COLS // 2
GROUP_CHUNKS = GROUPS // CHUNK_GROUPS
DIAG = GROUP_CHUNKS

T_SLOTS = 3
PROD_SLOTS = 4
Q_SLOTS = 3
S_SLOTS = 2
R_SLOTS = 3
RAW_SLOTS = 3
HI_SLOTS = 2
STRIP = 32
FILL_TILES = 64
FILLS = 4


def make_plan():
    steps, first = [], {}
    for n in range(COUPLES):
        first[n] = len(steps)
        if n % 2:
            steps.append(("diag", n - 1, n))
        steps += [("group", m, n) for m in range(n)]
    group_step = [k for k, s in enumerate(steps) if s[0] == "group"]
    last_use = {}
    for k, (kind, m, n) in enumerate(steps):
        last_use[n] = k
        if kind == "diag":
            last_use[m] = k
    couples_at = {k: [] for k in range(len(steps))}
    late_couples_at = {k: [] for k in range(len(steps))}
    for n in range(COUPLES):
        at = first[max(n - 1, 0)] if n < 9 else first[n] - 10
        couples_at[at].append(n)
        late_couples_at[at + (1 if n > 7 else 0)].append(n)
    order = [0, DIAG] + list(range(1, GROUP_CHUNKS))
    chunks_at = {k: [] for k in range(len(steps))}
    late_chunks_at = {k: [] for k in range(len(steps))}
    for c in order:
        at = 0 if c in (0, DIAG) else group_step[c * CHUNK_GROUPS] - (8 if c < R_SLOTS else 14)
        chunks_at[at].append(c)
        late_chunks_at[at + 3 if at else 0].append(c)
    return steps, group_step, last_use, couples_at, late_couples_at, chunks_at, late_chunks_at, order


(STEPS, GROUP_STEP, LAST_USE, COUPLES_AT, LATE_COUPLES_AT, CHUNKS_AT, LATE_CHUNKS_AT,
 CHUNK_ORDER) = make_plan()
N_STEPS = len(STEPS)
BATCHES = N_STEPS // 2
FILL_BATCHES = FILL_TILES // 4
LAG = 3


def pair_index(i, j):
    return i * FIELDS - i * (i + 1) // 2 + j - i - 1


def chunk_pairs():
    return [pair_index(2 * m + half, 2 * n + jj)
            for kind, m, n in STEPS if kind == "group" for jj in range(2) for half in range(2)]


def diag_pairs():
    return [pair_index(2 * m, 2 * m + 1) for m in range(COUPLES)]


def slot_pairs():
    rows = [PAIRS] * (FILLS * P)
    for k, (kind, m, n) in enumerate(STEPS):
        for jj in range(2):
            tile = 2 * k + jj
            row = tile // FILL_TILES * P + STRIP * (tile % 4) + 2 * (tile % FILL_TILES // 4)
            if kind == "group":
                rows[row] = pair_index(2 * m, 2 * n + jj)
                rows[row + 1] = pair_index(2 * m + 1, 2 * n + jj)
            else:
                c = (m, n)[jj]
                rows[row] = pair_index(2 * c, 2 * c + 1)
    return rows


def build(nc, ids, tables, k_chunks, w_slots, b_pair, w1, b1, w2, b2, w3, dense_t, out):
    with ExitStack() as ctx:
        def sb(name, shape, dt=F32):
            return ctx.enter_context(nc.sbuf_tensor(name, shape, dt))

        def sem(name):
            return ctx.enter_context(nc.semaphore(name))

        ids_sb = sb("ids_sb", [P, FIELDS, BT], I32)
        emb = sb("emb", [P, BT, FIELDS * D])
        et = sb("et", [P, COUPLES, BATCH])
        split = sb("split", [P, S_SLOTS, 2, BATCH], F32R)
        q = sb("q", [P, Q_SLOTS, 2, 2, BATCH], F32R)
        raw = sb("raw", [P, RAW_SLOTS, HALF_COLS])
        khi = sb("khi", [P, HI_SLOTS, HALF_COLS], F32R)
        r = sb("r", [P, R_SLOTS, CHUNK_COLS], F32R)
        rdiag = sb("rdiag", [P, CHUNK_COLS], F32R)
        prod = sb("prod", [P, PROD_SLOTS, 2, BATCH])
        pij = sb("pij", [P, FILLS, BATCH])
        ident = sb("ident", [P, P])
        sel = sb("sel", [P, 2 * STRIP - 2])
        w_sb = sb("w_sb", [P, 2, FILLS * P])
        bp_sb = sb("bp_sb", [P, 2])
        w1_sb = sb("w1_sb", [P, 2, H1])
        w1d_sb = sb("w1d_sb", [DENSE, H1])
        b1_sb = sb("b1_sb", [P, H1 // P])
        w2_sb = sb("w2_sb", [P, H1 // P, H2])
        b2_sb = sb("b2_sb", [P, H2 // P])
        w3_sb = sb("w3_sb", [P, H2 // P])
        dense_sb = sb("dense_sb", [DENSE, BATCH])
        wc = sb("wc", [P, FILLS, H1])
        bc = sb("bc", [P, H1 // P])
        y_sb = sb("y_sb", [1, BATCH])
        h1 = emb[:, 0, :].rearrange("p (m b) -> p m b", b=BATCH)
        h2 = emb[:, 1, 0:2 * BATCH].rearrange("p (m b) -> p m b", b=BATCH)

        ps = ctx.enter_context(nc.psum_tensor("ps", [P, 8, BATCH], F32))

        def t_tile(k):
            s = k % T_SLOTS
            return ps[:, 2 * s:2 * s + 2, :]

        ACC, TP = 6, 7
        H1_BANK = (4, 5, 0, 1)
        H2_BANK = (2, 3)

        ids_loaded = sem("ids_loaded")
        weights_loaded = sem("weights_loaded")
        mlp_loaded = sem("mlp_loaded")
        gathered = [sem(f"gathered{m}") for m in range(COUPLES)]
        raw_loaded = [sem(f"raw_loaded{s}") for s in range(RAW_SLOTS)]
        r_spread = [sem(f"r_spread{s}") for s in range(R_SLOTS)]
        diag_spread = sem("diag_spread")
        q_spread = [sem(f"q_spread{s}") for s in range(Q_SLOTS)]
        consts_zeroed = sem("consts_zeroed")
        ident_ready = sem("ident_ready")
        sel_ready = sem("sel_ready")
        wc_summed = sem("wc_summed")
        wc_ready = sem("wc_ready")
        bc_summed = sem("bc_summed")
        bc_ready = sem("bc_ready")
        transposed = sem("transposed")
        et_ready = sem("et_ready")
        q_hi_ready = sem("q_hi_ready")
        q_lo_ready = sem("q_lo_ready")
        k_hi_ready = sem("k_hi_ready")
        k_lo_ready = sem("k_lo_ready")
        t_ready = sem("t_ready")
        prod_ready = sem("prod_ready")
        pairs_summed = sem("pairs_summed")
        pij_ready = sem("pij_ready")
        h1_summed = sem("h1_summed")
        h1_ready = [sem(f"h1_ready{m}") for m in range(H1 // P)]
        h2_summed = sem("h2_summed")
        h2_ready = [sem(f"h2_ready{m}") for m in range(H2 // P)]
        y_summed = sem("y_summed")
        y_ready = sem("y_ready")
        stored = sem("stored")

        place = {c: s for s, c in enumerate(CHUNK_ORDER)}

        def wait_chunk_spread(eng, c):
            if c == DIAG:
                eng.wait_ge(diag_spread, 64)
            else:
                eng.wait_ge(r_spread[c % R_SLOTS], 64 * (c // R_SLOTS + 1))

        def wait_q_spread(eng, n):
            eng.wait_ge(q_spread[n % Q_SLOTS], 64 * (n // Q_SLOTS + 1))

        block = ctx.enter_context(nc.Block())

        @block.sync
        def _(sp):
            def load_chunk(s):
                if s >= RAW_SLOTS:
                    wait_chunk_spread(sp, CHUNK_ORDER[s - RAW_SLOTS])
                sp.dma_start(raw[:, s % RAW_SLOTS, :], k_chunks[CHUNK_ORDER[s]]).then_inc(
                    raw_loaded[s % RAW_SLOTS], 16)

            def spread_chunk(c):
                s = place[c]
                sp.wait_ge(k_lo_ready, s + 1)
                if c != DIAG and c >= R_SLOTS:
                    sp.wait_ge(t_ready, GROUP_STEP[(c - R_SLOTS + 1) * CHUNK_GROUPS - 1] + 1)
                dst = rdiag[:, :] if c == DIAG else r[:, c % R_SLOTS, :]
                done = diag_spread if c == DIAG else r_spread[c % R_SLOTS]
                for row, src in ((0, khi[:, s % HI_SLOTS, :].bitcast(F32)), (D, raw[:, s % RAW_SLOTS, :])):
                    for half in range(2):
                        sp.dma_start(dst[row:row + D, half * HALF_COLS:(half + 1) * HALF_COLS].bitcast(F32),
                                     src[half * D:(half + 1) * D, :]).then_inc(done, 16)

            def spread_couple(n):
                sp.wait_ge(q_lo_ready, n + 1)
                if n >= Q_SLOTS:
                    sp.wait_ge(t_ready, LAST_USE[n - Q_SLOTS] + 1)
                for field in range(2):
                    for half in range(2):
                        sp.dma_start(
                            q[half * D:(half + 1) * D, n % Q_SLOTS, field, :, :].bitcast(F32),
                            split[field * D:(field + 1) * D, n % S_SLOTS, :, :].bitcast(F32),
                        ).then_inc(q_spread[n % Q_SLOTS], 16)

            sp.dma_start(ids_sb[:, :, :], ids).then_inc(ids_loaded, 16)
            for s in range(2):
                load_chunk(s)
            sp.dma_start(w_sb[:, :, :], w_slots).then_inc(weights_loaded, 16)
            sp.dma_start(w1_sb[:, :, :], w1[0:D1, :].rearrange("(o p) m -> p o m", p=P)).then_inc(weights_loaded, 16)
            sp.dma_start(bp_sb[:, :], b_pair).then_inc(weights_loaded, 16)
            sp.dma_start(b1_sb[:, :], b1).then_inc(weights_loaded, 16)
            load_chunk(2)
            sp.dma_start(w1d_sb[:, :], w1[D1:D1 + DENSE, :]).then_inc(mlp_loaded, 16)
            sp.dma_start(dense_sb[:, :], dense_t).then_inc(mlp_loaded, 16)
            sp.dma_start(w2_sb[:, :, :], w2.rearrange("(k p) m -> p k m", p=P)).then_inc(mlp_loaded, 16)
            sp.dma_start(b2_sb[:, :], b2).then_inc(mlp_loaded, 16)
            sp.dma_start(w3_sb[:, :], w3).then_inc(mlp_loaded, 16)
            for c in LATE_CHUNKS_AT[0]:
                spread_chunk(c)
            for k in range(N_STEPS):
                for n in LATE_COUPLES_AT[k]:
                    spread_couple(n)
                for c in LATE_CHUNKS_AT[k]:
                    if k:
                        spread_chunk(c)
                    s = place[c] - 1 + RAW_SLOTS
                    if RAW_SLOTS <= s < len(CHUNK_ORDER):
                        load_chunk(s)
            sp.wait_ge(y_ready, 1)
            sp.dma_start(out.rearrange("b o -> o b"), y_sb[:, :]).then_inc(stored, 16)
            sp.wait_ge(stored, 16)

        @block.gpsimd
        def _(pool):
            nc.gpsimd.memset(ident[:, :], 0.0).then_inc(consts_zeroed, 1)
            pool.wait_ge(consts_zeroed, 1)
            nc.gpsimd.affine_select(out=ident[:, :], in_=ident[:, :], compare_op=ALU.not_equal, fill=1.0,
                                    base=0, pattern=[[-1, P]], channel_multiplier=1).then_inc(ident_ready, 1)
            pool.wait_ge(ids_loaded, 16)
            for f in range(FIELDS):
                for bt in range(BT):
                    pool.indirect_dma_start(
                        emb[:, bt, f * D:(f + 1) * D], None, tables[f],
                        bass.IndirectOffsetOnAxis(ids_sb[:, f, bt:bt + 1].bitcast(U32), 0),
                    ).then_inc(gathered[f // 2], 16)

        @block.scalar
        def _(act):
            def chunk_hi(c):
                s = place[c]
                act.wait_ge(raw_loaded[s % RAW_SLOTS], 16 * (s // RAW_SLOTS + 1))
                if s >= HI_SLOTS:
                    wait_chunk_spread(act, CHUNK_ORDER[s - HI_SLOTS])
                nc.scalar.activation(khi[:, s % HI_SLOTS, :], raw[:, s % RAW_SLOTS, :],
                                     ACT.Copy).then_inc(k_hi_ready, 1)

            def couple_hi(n):
                act.wait_ge(transposed, n + 1)
                nc.scalar.activation(et[:, n, :], ps[:, TP, :], ACT.Copy).then_inc(et_ready, 1)
                if n >= S_SLOTS:
                    wait_q_spread(act, n - S_SLOTS)
                nc.scalar.activation(split[:, n % S_SLOTS, 0, :], ps[:, TP, :], ACT.Copy).then_inc(q_hi_ready, 1)

            def take_pairs(f):
                act.wait_ge(pairs_summed, FILL_BATCHES * (f + 1))
                nc.scalar.activation(pij[:, f, :], ps[:, ACC, :], ACT.Copy).then_inc(pij_ready, 1)

            for c in CHUNKS_AT[0]:
                chunk_hi(c)
            for k in range(N_STEPS):
                for n in COUPLES_AT[k]:
                    couple_hi(n)
                    if n < 2:
                        for f in (2 * n, 2 * n + 1):
                            act.wait_ge(wc_summed, f + 1)
                            nc.scalar.activation(wc[:, f, :], ps[:, f, :], ACT.Copy).then_inc(wc_ready, 1)
                for c in CHUNKS_AT[k]:
                    if k:
                        chunk_hi(c)
                b = (k - LAG) // 2
                if k % 2 and k > LAG and (b + 1) % FILL_BATCHES == 0:
                    take_pairs(b // FILL_BATCHES)
            take_pairs(FILLS - 1)
            act.wait_ge(bc_ready, 1)
            for m in range(0, H1 // P, 2):
                act.wait_ge(h1_summed, m + 1)
                nc.scalar.activation(h1[:, m, :], ps[:, H1_BANK[m], :], ACT.Relu,
                                     bias=bc[:, m:m + 1]).then_inc(h1_ready[m], 1)
            act.wait_ge(mlp_loaded, 80)
            act.wait_ge(h2_summed, 1)
            nc.scalar.activation(h2[:, 0, :], ps[:, H2_BANK[0], :], ACT.Relu,
                                 bias=b2_sb[:, 0:1]).then_inc(h2_ready[0], 1)
            act.wait_ge(y_summed, 1)
            nc.scalar.activation(y_sb[:, :], ps[0:1, TP, :], ACT.Copy).then_inc(y_ready, 1)

        @block.vector
        def _(dve):
            def chunk_lo(c):
                s = place[c]
                dve.wait_ge(k_hi_ready, s + 1)
                nc.vector.tensor_tensor(raw[:, s % RAW_SLOTS, :], raw[:, s % RAW_SLOTS, :],
                                        khi[:, s % HI_SLOTS, :].bitcast(F32),
                                        ALU.subtract).then_inc(k_lo_ready, 1)

            def couple_lo(n):
                dve.wait_ge(q_hi_ready, n + 1)
                nc.vector.tensor_tensor(split[:, n % S_SLOTS, 1, :], et[:, n, :],
                                        split[:, n % S_SLOTS, 0, :].bitcast(F32),
                                        ALU.subtract).then_inc(q_lo_ready, 1)

            def multiply(k):
                kind, m, n = STEPS[k]
                dve.wait_ge(t_ready, k + 1)
                if k >= PROD_SLOTS:
                    dve.wait_ge(pairs_summed, (k - PROD_SLOTS) // 2 + 1)
                p_i = et[:, m, :].unsqueeze(1).broadcast_to([P, 2, BATCH]) if kind == "group" else et[:, m:n + 1, :]
                nc.vector.tensor_tensor(prod[:, k % PROD_SLOTS, :, :], t_tile(k), p_i,
                                        ALU.mult).then_inc(prod_ready, 1)

            nc.vector.memset(sel[:, :], 0.0).then_inc(sel_ready, 1)
            dve.wait_ge(sel_ready, 1)
            nc.vector.memset(sel[0:D, STRIP - 2:STRIP - 1], 1.0).then_inc(sel_ready, 1)
            nc.vector.memset(sel[D:P, STRIP - 1:STRIP], 1.0).then_inc(sel_ready, 1)
            dve.wait_ge(bc_summed, 1)
            dve.wait_ge(weights_loaded, 64)
            nc.vector.tensor_tensor(bc[:, :], ps[:, 4, 0:H1 // P], b1_sb[:, :], ALU.add).then_inc(bc_ready, 1)
            for c in CHUNKS_AT[0]:
                chunk_lo(c)
            for k in range(N_STEPS):
                for n in LATE_COUPLES_AT[k]:
                    couple_lo(n)
                for c in LATE_CHUNKS_AT[k]:
                    if k:
                        chunk_lo(c)
                multiply(k)
            for m in range(1, H1 // P, 2):
                dve.wait_ge(h1_summed, m + 1)
                dve.wait_ge(bc_ready, 1)
                nc.vector.tensor_scalar(h1[:, m, :], ps[:, H1_BANK[m], :], bc[:, m:m + 1], 0.0,
                                        ALU.add, ALU.max).then_inc(h1_ready[m], 1)
            dve.wait_ge(mlp_loaded, 80)
            dve.wait_ge(h2_summed, 2)
            nc.vector.tensor_scalar(h2[:, 1, :], ps[:, H2_BANK[1], :], b2_sb[:, 1:2], 0.0,
                                    ALU.add, ALU.max).then_inc(h2_ready[1], 1)

        @block.tensor
        def _(pe):
            def transpose_couple(n):
                pe.wait_ge(gathered[n], 16 * 2 * BT)
                if n >= 1:
                    pe.wait_ge(q_hi_ready, n)
                for bt in range(BT):
                    last = nc.tensor.transpose(ps[:, TP, bt * P:(bt + 1) * P],
                                               emb[:, bt, 2 * n * D:2 * (n + 1) * D], ident[:, :])
                last.then_inc(transposed, 1)

            def contract(k):
                kind, m, n = STEPS[k]
                if kind == "group":
                    g = GROUP_STEP.index(k)
                    c = g // CHUNK_GROUPS
                    at = g % CHUNK_GROUPS * GROUP_COLS
                    weights = [r[:, c % R_SLOTS, at + jj * P:at + (jj + 1) * P] for jj in range(2)]
                    right = [q[:, n % Q_SLOTS, jj] for jj in range(2)]
                else:
                    c = DIAG
                    weights = [rdiag[:, x * P:(x + 1) * P] for x in (m, n)]
                    right = [q[:, x % Q_SLOTS, 1] for x in (m, n)]
                    wait_q_spread(pe, m)
                wait_chunk_spread(pe, c)
                wait_q_spread(pe, n)
                if k >= T_SLOTS:
                    pe.wait_ge(prod_ready, k - T_SLOTS + 1)
                for jj in range(2):
                    for part in range(2):
                        last = nc.tensor.matmul(t_tile(k)[:, jj, :], weights[jj], right[jj][:, part, :],
                                                start=(part == 0), stop=(part == 1))
                last.then_inc(t_ready, 1)

            def sum_pairs(b):
                pe.wait_ge(prod_ready, 2 * b + 2)
                at = b % FILL_BATCHES
                if b >= FILL_BATCHES and at == 0:
                    pe.wait_ge(pij_ready, b // FILL_BATCHES)
                for x in range(4):
                    k = 2 * b + x // 2
                    last = nc.tensor.matmul(ps[STRIP * x:STRIP * (x + 1), ACC, :],
                                            sel[:, STRIP - 2 - 2 * at:2 * STRIP - 2 - 2 * at],
                                            prod[:, k % PROD_SLOTS, x % 2, :],
                                            start=(at == 0), stop=(at == FILL_BATCHES - 1))
                last.then_inc(pairs_summed, 1)

            def fold_weights(f):
                for o in range(2):
                    last = nc.tensor.matmul(ps[:, f, :], w_sb[:, o, f * P:(f + 1) * P], w1_sb[:, o, :],
                                            start=(o == 0), stop=(o == 1))
                last.then_inc(wc_summed, 1)

            pe.wait_ge(weights_loaded, 64)
            for m in range(H1 // P):
                for o in range(2):
                    last = nc.tensor.matmul(ps[:, 4, m:m + 1], w1_sb[:, o, m * P:(m + 1) * P], bp_sb[:, o:o + 1],
                                            start=(o == 0), stop=(o == 1))
            last.then_inc(bc_summed, 1)
            for f in range(2):
                fold_weights(f)
            pe.wait_ge(ident_ready, 1)
            pe.wait_ge(sel_ready, 3)
            for k in range(N_STEPS):
                for n in COUPLES_AT[k]:
                    transpose_couple(n)
                    if n == 0:
                        for f in range(2, FILLS):
                            fold_weights(f)
                if k == 0:
                    pe.wait_ge(wc_ready, FILLS)
                if k == 2:
                    pe.wait_ge(bc_ready, 1)
                contract(k)
                if k % 2 and k >= LAG:
                    sum_pairs((k - LAG) // 2)

            def h1_early(m):
                nc.tensor.matmul(ps[:, H1_BANK[m], :], w1d_sb[:, m * P:(m + 1) * P], dense_sb[:, :],
                                 start=True, stop=False)
                for f in range(FILLS - 1):
                    nc.tensor.matmul(ps[:, H1_BANK[m], :], wc[:, f, m * P:(m + 1) * P], pij[:, f, :],
                                     start=False, stop=False)

            pe.wait_ge(mlp_loaded, 80)
            pe.wait_ge(pij_ready, FILLS - 1)
            pe.wait_ge(prod_ready, N_STEPS - 2)
            for m in (0, 1):
                h1_early(m)
            sum_pairs(BATCHES - 1)
            for m in (2, 3):
                h1_early(m)
            pe.wait_ge(pij_ready, FILLS)
            for m in range(H1 // P):
                nc.tensor.matmul(ps[:, H1_BANK[m], :], wc[:, FILLS - 1, m * P:(m + 1) * P], pij[:, FILLS - 1, :],
                                 start=False, stop=True).then_inc(h1_summed, 1)
            for kk in range(H1 // P):
                pe.wait_ge(h1_ready[kk], 1)
                for m in range(H2 // P):
                    mm = nc.tensor.matmul(ps[:, H2_BANK[m], :], w2_sb[:, kk, m * P:(m + 1) * P], h1[:, kk, :],
                                          start=(kk == 0), stop=(kk == H1 // P - 1))
                    if kk == H1 // P - 1:
                        mm.then_inc(h2_summed, 1)
            for kk in range(H2 // P):
                pe.wait_ge(h2_ready[kk], 1)
                mm = nc.tensor.matmul(ps[0:1, TP, :], w3_sb[:, kk:kk + 1], h2[:, kk, :],
                                      start=(kk == 0), stop=(kk == H2 // P - 1))
            mm.then_inc(y_summed, 1)


def kernel(**inputs):
    import numpy as _np
    import concourse.bacc as _bacc
    from concourse import mybir as _mybir
    from concourse.bass_utils import run_bass_kernel_spmd as _run

    a = {name: _np.asarray(x) for name, x in inputs.items()}
    k = a["L0_rec_kernel"]
    group_part = k[:, _np.array(chunk_pairs()), :].reshape(D, GROUP_CHUNKS, 2, HALF_COLS)
    diag_part = _np.concatenate([k[:, _np.array(diag_pairs()), :], _np.zeros((D, COUPLES, D), k.dtype)], axis=2)
    k_chunks = _np.concatenate([group_part, diag_part.reshape(D, 1, 2, HALF_COLS)], axis=1)
    k_chunks = k_chunks.transpose(1, 2, 0, 3).reshape(GROUP_CHUNKS + 1, P, HALF_COLS)
    w = _np.concatenate([a["L0_rec_W"], _np.zeros((D1, 1), k.dtype)], axis=1)[:, _np.array(slot_pairs())]
    arrays = {
        "ids": a["ids"].reshape(BT, P, FIELDS).transpose(1, 2, 0),
        "k_chunks": k_chunks,
        "w_slots": w.reshape(2, P, FILLS * P).transpose(1, 0, 2),
        "b_pair": a["L0_rec_b"].reshape(2, P).T,
        "w1": a["W_top1"],
        "b1": a["b_top1"].reshape(H1 // P, P).T,
        "w2": a["W_top2"],
        "b2": a["b_top2"].reshape(H2 // P, P).T,
        "w3": a["W_top3"].reshape(H2 // P, P).T,
        "dense_t": a["dense_ctx"].T,
    }
    for f in range(FIELDS):
        arrays[f"tbl_{f}"] = a[f"tbl_{f}"]
    arrays = {f"in_{name}": _np.ascontiguousarray(x) for name, x in arrays.items()}

    nc = _bacc.Bacc("TRN2", target_bir_lowering=False, num_devices=1)
    dram = {name[3:]: nc.dram_tensor(name, x.shape, _mybir.dt.from_np(x.dtype), kind="ExternalInput").ap()
            for name, x in arrays.items()}
    out = nc.dram_tensor("out_0", (BATCH, 1), _mybir.dt.float32, kind="ExternalOutput").ap()
    tables = [dram.pop(f"tbl_{f}") for f in range(FIELDS)]
    build(nc, tables=tables, out=out, **dram)
    result = _run(nc, [arrays], core_ids=[0])
    return result.results[0]["out_0"]
```

```python
from contextlib import ExitStack

import numpy as np

import concourse.bass as bass
from concourse import mybir

F32 = mybir.dt.float32
F32R = mybir.dt.float32r
I32 = mybir.dt.int32
U32 = mybir.dt.uint32
ALU = mybir.AluOpType
ACT = mybir.ActivationFunctionType

P = 128
BATCH = 512
BT = BATCH // P
FIELDS = 32
D = 64
COUPLES = FIELDS // 2
PAIRS = FIELDS * (FIELDS - 1) // 2
D1 = 256
DENSE = 16
H1 = 512
H2 = 256
GROUPS = COUPLES * (COUPLES - 1) // 2
GROUP_COLS = 4 * D
CHUNK_GROUPS = 8
CHUNK_COLS = CHUNK_GROUPS * GROUP_COLS
HALF_COLS = CHUNK_COLS // 2
GROUP_CHUNKS = GROUPS // CHUNK_GROUPS
DIAG = GROUP_CHUNKS

LOOKED_UP = 2
LOOKUP_ROWS = (1000, 1000, 1000, 1250)
LOOKUP_PARTS = 125
LOOKUP_MAX = max(LOOKUP_ROWS) // LOOKUP_PARTS

T_SLOTS = 3
PROD_SLOTS = 4
Q_SLOTS = 3
S_SLOTS = 2
R_SLOTS = 3
ONEHOT_SLOTS = 8
RAW_SLOTS = 3
HI_SLOTS = 2
STRIP = 32
FILL_TILES = 64
FILLS = 4


def make_plan():
    steps, first = [], {}
    for n in range(COUPLES):
        first[n] = len(steps)
        block = [("group", m, n) for m in range(n)]
        if n % 2:
            block.insert(1 if n == 1 else 0, ("diag", n - 1, n))
        steps += block
    group_step = [k for k, s in enumerate(steps) if s[0] == "group"]
    last_use = {}
    for k, (kind, m, n) in enumerate(steps):
        last_use[n] = k
        if kind == "diag":
            last_use[m] = k
    couples_at = {k: [] for k in range(len(steps))}
    late_couples_at = {k: [] for k in range(len(steps))}
    for n in range(COUPLES):
        at = 0 if n < 3 else 1 if n == 3 else max(first[n] - (8 if n < 9 else 10), 2)
        couples_at[at].append(n)
        late_couples_at[at + (1 if n > 7 else 0)].append(n)
    order = [0, DIAG] + list(range(1, GROUP_CHUNKS))
    chunks_at = {k: [] for k in range(len(steps))}
    late_chunks_at = {k: [] for k in range(len(steps))}
    for c in order:
        at = 0 if c in (0, DIAG) else max(group_step[c * CHUNK_GROUPS] - (11 if c < R_SLOTS else 14), 1)
        chunks_at[at].append(c)
        late_chunks_at[at + 3 if at else 0].append(c)
    return steps, group_step, last_use, couples_at, late_couples_at, chunks_at, late_chunks_at, order


(STEPS, GROUP_STEP, LAST_USE, COUPLES_AT, LATE_COUPLES_AT, CHUNKS_AT, LATE_CHUNKS_AT,
 CHUNK_ORDER) = make_plan()
N_STEPS = len(STEPS)
BATCHES = N_STEPS // 2
FILL_BATCHES = FILL_TILES // 4
LAG = 3


def lookup_rows():
    part = np.arange(LOOKUP_PARTS)[:, None]
    return np.concatenate([part * (v // LOOKUP_PARTS) + np.arange(v // LOOKUP_PARTS)
                           for v in LOOKUP_ROWS], axis=1).astype(np.float32)


def pair_index(i, j):
    return i * FIELDS - i * (i + 1) // 2 + j - i - 1


def chunk_pairs():
    return [pair_index(2 * m + half, 2 * n + jj)
            for kind, m, n in STEPS if kind == "group" for jj in range(2) for half in range(2)]


def diag_pairs():
    return [pair_index(2 * m, 2 * m + 1) for m in range(COUPLES)]


def slot_pairs():
    rows = [PAIRS] * (FILLS * P)
    for k, (kind, m, n) in enumerate(STEPS):
        for jj in range(2):
            tile = 2 * k + jj
            row = tile // FILL_TILES * P + STRIP * (tile % 4) + 2 * (tile % FILL_TILES // 4)
            if kind == "group":
                rows[row] = pair_index(2 * m, 2 * n + jj)
                rows[row + 1] = pair_index(2 * m + 1, 2 * n + jj)
            else:
                c = (m, n)[jj]
                rows[row] = pair_index(2 * c, 2 * c + 1)
    return rows


def build(nc, ids, ids_t, row_numbers, tables, k_chunks, w_slots, b_pair, w1, b1, w2, b2, w3, dense_t, out):
    with ExitStack() as ctx:
        def sb(name, shape, dt=F32):
            return ctx.enter_context(nc.sbuf_tensor(name, shape, dt))

        def sem(name):
            return ctx.enter_context(nc.semaphore(name))

        ids_sb = sb("ids_sb", [P, FIELDS, BT], I32)
        emb = sb("emb", [P, BT, FIELDS * D])
        et = sb("et", [P, COUPLES, BATCH])
        split = sb("split", [P, S_SLOTS, 2, BATCH], F32R)
        q = sb("q", [P, Q_SLOTS, 2, 2, BATCH], F32R)
        raw = sb("raw", [P, RAW_SLOTS, HALF_COLS])
        khi = sb("khi", [P, HI_SLOTS, HALF_COLS], F32R)
        r = sb("r", [P, R_SLOTS, CHUNK_COLS], F32R)
        rdiag = sb("rdiag", [P, CHUNK_COLS], F32R)
        row_of = sb("row_of", [LOOKUP_PARTS, sum(LOOKUP_ROWS) // LOOKUP_PARTS])
        prod = sb("prod", [P, PROD_SLOTS, 2, BATCH])
        pij = sb("pij", [P, FILLS, BATCH])
        ident = sb("ident", [P, P])
        sel = sb("sel", [P, 2 * STRIP - 2])
        w_sb = sb("w_sb", [P, 2, FILLS * P])
        bp_sb = sb("bp_sb", [P, 2])
        w1_sb = sb("w1_sb", [P, 2, H1])
        w1d_sb = sb("w1d_sb", [DENSE, H1])
        b1_sb = sb("b1_sb", [P, H1 // P])
        w2_sb = sb("w2_sb", [P, H1 // P, H2])
        b2_sb = sb("b2_sb", [P, H2 // P])
        w3_sb = sb("w3_sb", [P, H2 // P])
        dense_sb = sb("dense_sb", [DENSE, BATCH])
        wc = sb("wc", [P, FILLS, H1])
        bc = sb("bc", [P, H1 // P])
        y_sb = sb("y_sb", [1, BATCH])
        tbl = emb[0:LOOKUP_PARTS, :, (FIELDS - LOOKUP_MAX) * D:]
        onehot = et[0:LOOKUP_PARTS, COUPLES - ONEHOT_SLOTS:, :]
        ids_all = pij[0:LOOKUP_PARTS, :, :].bitcast(I32)

        h1 = emb[:, 0, :].rearrange("p (m b) -> p m b", b=BATCH)
        h2 = emb[:, 1, 0:2 * BATCH].rearrange("p (m b) -> p m b", b=BATCH)

        ps = ctx.enter_context(nc.psum_tensor("ps", [P, 8, BATCH], F32))

        def t_tile(k):
            s = k % T_SLOTS
            return ps[:, 2 * s:2 * s + 2, :]

        ACC, TP = 6, 7
        COUPLE_BANK = (5,) + (TP,) * (COUPLES - 1)
        H1_BANK = (4, 5, 0, 1)
        H2_BANK = (2, 3)

        ids_loaded = sem("ids_loaded")
        weights_loaded = sem("weights_loaded")
        mlp_loaded = sem("mlp_loaded")
        gathered = [sem(f"gathered{m}") for m in range(COUPLES)]
        raw_loaded = [sem(f"raw_loaded{s}") for s in range(RAW_SLOTS)]
        r_spread = [sem(f"r_spread{s}") for s in range(R_SLOTS)]
        diag_spread = sem("diag_spread")
        q_spread = [sem(f"q_spread{s}") for s in range(Q_SLOTS)]
        lookup_loaded = [sem(f"lookup_loaded{m}") for m in range(LOOKED_UP)]
        onehot_ready = sem("onehot_ready")
        onehot_used = sem("onehot_used")
        consts_zeroed = sem("consts_zeroed")
        ident_ready = sem("ident_ready")
        sel_ready = sem("sel_ready")
        wc_summed = sem("wc_summed")
        wc_ready = sem("wc_ready")
        bc_summed = sem("bc_summed")
        bc_ready = sem("bc_ready")
        transposed = sem("transposed")
        et_ready = sem("et_ready")
        q_hi_ready = sem("q_hi_ready")
        q_lo_ready = sem("q_lo_ready")
        k_hi_ready = sem("k_hi_ready")
        k_lo_ready = sem("k_lo_ready")
        t_ready = sem("t_ready")
        prod_ready = sem("prod_ready")
        pairs_summed = sem("pairs_summed")
        pij_ready = sem("pij_ready")
        h1_summed = sem("h1_summed")
        h1_ready = [sem(f"h1_ready{m}") for m in range(H1 // P)]
        h2_summed = sem("h2_summed")
        h2_ready = [sem(f"h2_ready{m}") for m in range(H2 // P)]
        y_summed = sem("y_summed")
        y_ready = sem("y_ready")
        stored = sem("stored")

        place = {c: s for s, c in enumerate(CHUNK_ORDER)}

        def wait_chunk_spread(eng, c):
            if c == DIAG:
                eng.wait_ge(diag_spread, 64)
            else:
                eng.wait_ge(r_spread[c % R_SLOTS], 64 * (c // R_SLOTS + 1))

        def wait_q_spread(eng, n):
            eng.wait_ge(q_spread[n % Q_SLOTS], 64 * (n // Q_SLOTS + 1))

        def lookup_blocks(m):
            blocks = [v // LOOKUP_PARTS for v in LOOKUP_ROWS]
            return [(f, c, sum(blocks[:f]) + c) for c in range(LOOKUP_MAX) for f in (2 * m, 2 * m + 1)
                    if c < blocks[f]]

        lookup_order = [x for m in range(LOOKED_UP) for x in lookup_blocks(m)]

        block = ctx.enter_context(nc.Block())

        @block.sync
        def _(sp):
            def load_chunk(s):
                if s >= RAW_SLOTS:
                    wait_chunk_spread(sp, CHUNK_ORDER[s - RAW_SLOTS])
                sp.dma_start(raw[:, s % RAW_SLOTS, :], k_chunks[CHUNK_ORDER[s]]).then_inc(
                    raw_loaded[s % RAW_SLOTS], 16)

            def spread_chunk(c):
                s = place[c]
                sp.wait_ge(k_lo_ready, s + 1)
                if c != DIAG and c >= R_SLOTS:
                    sp.wait_ge(t_ready, GROUP_STEP[(c - R_SLOTS + 1) * CHUNK_GROUPS - 1] + 1)
                dst = rdiag[:, :] if c == DIAG else r[:, c % R_SLOTS, :]
                done = diag_spread if c == DIAG else r_spread[c % R_SLOTS]
                for row, src in ((0, khi[:, s % HI_SLOTS, :].bitcast(F32)), (D, raw[:, s % RAW_SLOTS, :])):
                    for half in range(2):
                        sp.dma_start(dst[row:row + D, half * HALF_COLS:(half + 1) * HALF_COLS].bitcast(F32),
                                     src[half * D:(half + 1) * D, :]).then_inc(done, 16)

            def spread_couple(n):
                sp.wait_ge(q_lo_ready, n + 1)
                if n >= Q_SLOTS:
                    sp.wait_ge(t_ready, LAST_USE[n - Q_SLOTS] + 1)
                for field in range(2):
                    for half in range(2):
                        sp.dma_start(
                            q[half * D:(half + 1) * D, n % Q_SLOTS, field, :, :].bitcast(F32),
                            split[field * D:(field + 1) * D, n % S_SLOTS, :, :].bitcast(F32),
                        ).then_inc(q_spread[n % Q_SLOTS], 16)

            sp.dma_start(ids_sb[:, :, :], ids).then_inc(ids_loaded, 16)
            for m in range(LOOKED_UP):
                sp.dma_start(ids_all[:, 2 * m:2 * m + 2, :],
                             ids_t[2 * m:2 * m + 2, :].unsqueeze(0).broadcast_to([LOOKUP_PARTS, 2, BATCH])
                             ).then_inc(lookup_loaded[m], 16)
                if m == 0:
                    sp.dma_start(row_of[:, :], row_numbers).then_inc(lookup_loaded[m], 16)
                for f in (2 * m, 2 * m + 1):
                    sp.dma_start(tbl[:, f, 0:LOOKUP_ROWS[f] // LOOKUP_PARTS * D],
                                 tables[f].rearrange("(p c) d -> p (c d)", p=LOOKUP_PARTS)
                                 ).then_inc(lookup_loaded[m], 16)
            for s in range(2):
                load_chunk(s)
            sp.dma_start(w_sb[:, :, :], w_slots).then_inc(weights_loaded, 16)
            sp.dma_start(w1_sb[:, :, :], w1[0:D1, :].rearrange("(o p) m -> p o m", p=P)).then_inc(weights_loaded, 16)
            sp.dma_start(bp_sb[:, :], b_pair).then_inc(weights_loaded, 16)
            sp.dma_start(b1_sb[:, :], b1).then_inc(weights_loaded, 16)
            load_chunk(2)
            sp.dma_start(w1d_sb[:, :], w1[D1:D1 + DENSE, :]).then_inc(mlp_loaded, 16)
            sp.dma_start(dense_sb[:, :], dense_t).then_inc(mlp_loaded, 16)
            sp.dma_start(w2_sb[:, :, :], w2.rearrange("(k p) m -> p k m", p=P)).then_inc(mlp_loaded, 16)
            sp.dma_start(b2_sb[:, :], b2).then_inc(mlp_loaded, 16)
            sp.dma_start(w3_sb[:, :], w3).then_inc(mlp_loaded, 16)
            spread_chunk(CHUNK_ORDER[0])
            spread_couple(0)
            spread_couple(1)
            spread_chunk(DIAG)
            for k in range(N_STEPS):
                for n in LATE_COUPLES_AT[k]:
                    if n >= LOOKED_UP:
                        spread_couple(n)
                for c in LATE_CHUNKS_AT[k]:
                    if k:
                        spread_chunk(c)
                    s = place[c] - 1 + RAW_SLOTS
                    if RAW_SLOTS <= s < len(CHUNK_ORDER):
                        load_chunk(s)
            sp.wait_ge(y_ready, 1)
            sp.dma_start(out.rearrange("b o -> o b"), y_sb[:, :]).then_inc(stored, 16)
            sp.wait_ge(stored, 16)

        @block.gpsimd
        def _(pool):
            nc.gpsimd.memset(ident[:, :], 0.0).then_inc(consts_zeroed, 1)
            pool.wait_ge(consts_zeroed, 1)
            nc.gpsimd.affine_select(out=ident[:, :], in_=ident[:, :], compare_op=ALU.not_equal, fill=1.0,
                                    base=0, pattern=[[-1, P]], channel_multiplier=1).then_inc(ident_ready, 1)
            pool.wait_ge(ids_loaded, 16)
            for f in range(2 * LOOKED_UP, FIELDS):
                if f == FIELDS - LOOKUP_MAX:
                    pool.wait_ge(onehot_used, len(lookup_order))
                for bt in range(BT):
                    pool.indirect_dma_start(
                        emb[:, bt, f * D:(f + 1) * D], None, tables[f],
                        bass.IndirectOffsetOnAxis(ids_sb[:, f, bt:bt + 1].bitcast(U32), 0),
                    ).then_inc(gathered[f // 2], 16)

        @block.scalar
        def _(act):
            def chunk_hi(c):
                s = place[c]
                act.wait_ge(raw_loaded[s % RAW_SLOTS], 16 * (s // RAW_SLOTS + 1))
                if s >= HI_SLOTS:
                    wait_chunk_spread(act, CHUNK_ORDER[s - HI_SLOTS])
                nc.scalar.activation(khi[:, s % HI_SLOTS, :], raw[:, s % RAW_SLOTS, :],
                                     ACT.Copy).then_inc(k_hi_ready, 1)

            def couple_hi(n):
                if n < LOOKED_UP:
                    act.wait_ge(onehot_used, sum(len(lookup_blocks(m)) for m in range(n + 1)))
                else:
                    act.wait_ge(transposed, n + 1 - LOOKED_UP)
                nc.scalar.activation(et[:, n, :], ps[:, COUPLE_BANK[n], :], ACT.Copy).then_inc(et_ready, 1)
                if n >= S_SLOTS:
                    wait_q_spread(act, n - S_SLOTS)
                nc.scalar.activation(split[:, n % S_SLOTS, 0, :], ps[:, COUPLE_BANK[n], :],
                                     ACT.Copy).then_inc(q_hi_ready, 1)

            def take_pairs(f):
                act.wait_ge(pairs_summed, FILL_BATCHES * (f + 1))
                nc.scalar.activation(pij[:, f, :], ps[:, ACC, :], ACT.Copy).then_inc(pij_ready, 1)

            for c in CHUNKS_AT[0]:
                chunk_hi(c)
            for k in range(N_STEPS):
                for n in COUPLES_AT[k]:
                    couple_hi(n)
                    if n == 1:
                        for f in range(FILLS):
                            act.wait_ge(wc_summed, f + 1)
                            nc.scalar.activation(wc[:, f, :], ps[:, f, :], ACT.Copy).then_inc(wc_ready, 1)
                for c in CHUNKS_AT[k]:
                    if k:
                        chunk_hi(c)
                b = (k - LAG) // 2
                if k % 2 and k > LAG and (b + 1) % FILL_BATCHES == 0:
                    take_pairs(b // FILL_BATCHES)
            take_pairs(FILLS - 1)
            act.wait_ge(bc_ready, 1)
            for m in range(0, H1 // P, 2):
                act.wait_ge(h1_summed, m + 1)
                nc.scalar.activation(h1[:, m, :], ps[:, H1_BANK[m], :], ACT.Relu,
                                     bias=bc[:, m:m + 1]).then_inc(h1_ready[m], 1)
            act.wait_ge(mlp_loaded, 80)
            act.wait_ge(h2_summed, 1)
            nc.scalar.activation(h2[:, 0, :], ps[:, H2_BANK[0], :], ACT.Relu,
                                 bias=b2_sb[:, 0:1]).then_inc(h2_ready[0], 1)
            act.wait_ge(y_summed, 1)
            nc.scalar.activation(y_sb[:, :], ps[0:1, TP, :], ACT.Copy).then_inc(y_ready, 1)

        @block.vector
        def _(dve):
            def chunk_lo(c):
                s = place[c]
                dve.wait_ge(k_hi_ready, s + 1)
                nc.vector.tensor_tensor(raw[:, s % RAW_SLOTS, :], raw[:, s % RAW_SLOTS, :],
                                        khi[:, s % HI_SLOTS, :].bitcast(F32),
                                        ALU.subtract).then_inc(k_lo_ready, 1)

            def couple_lo(n):
                dve.wait_ge(q_hi_ready, n + 1)
                nc.vector.tensor_tensor(split[:, n % S_SLOTS, 1, :], et[:, n, :],
                                        split[:, n % S_SLOTS, 0, :].bitcast(F32),
                                        ALU.subtract).then_inc(q_lo_ready, 1)

            def multiply(k):
                kind, m, n = STEPS[k]
                dve.wait_ge(t_ready, k + 1)
                if k >= PROD_SLOTS:
                    dve.wait_ge(pairs_summed, (k - PROD_SLOTS) // 2 + 1)
                p_i = et[:, m, :].unsqueeze(1).broadcast_to([P, 2, BATCH]) if kind == "group" else et[:, m:n + 1, :]
                nc.vector.tensor_tensor(prod[:, k % PROD_SLOTS, :, :], t_tile(k), p_i,
                                        ALU.mult).then_inc(prod_ready, 1)

            nc.vector.memset(sel[:, :], 0.0).then_inc(sel_ready, 1)
            dve.wait_ge(sel_ready, 1)
            nc.vector.memset(sel[0:D, STRIP - 2:STRIP - 1], 1.0).then_inc(sel_ready, 1)
            nc.vector.memset(sel[D:P, STRIP - 1:STRIP], 1.0).then_inc(sel_ready, 1)
            for i, (f, c, row) in enumerate(lookup_order):
                if i >= ONEHOT_SLOTS:
                    dve.wait_ge(onehot_used, i - ONEHOT_SLOTS + 1)
                dve.wait_ge(lookup_loaded[f // 2], 64 if f < 2 else 48)
                nc.vector.tensor_scalar(onehot[:, i % ONEHOT_SLOTS, :], ids_all[:, f, :],
                                        row_of[:, row:row + 1], None, ALU.is_equal).then_inc(onehot_ready, 1)
                if (f, c) == (2, 1):
                    chunk_lo(CHUNK_ORDER[0])
                if (f, c) == (2, 4):
                    couple_lo(0)
            couple_lo(1)
            chunk_lo(DIAG)
            dve.wait_ge(bc_summed, 1)
            dve.wait_ge(weights_loaded, 64)
            nc.vector.tensor_tensor(bc[:, :], ps[:, 4, 0:H1 // P], b1_sb[:, :], ALU.add).then_inc(bc_ready, 1)
            for k in range(N_STEPS):
                for n in LATE_COUPLES_AT[k]:
                    if n >= LOOKED_UP:
                        couple_lo(n)
                for c in LATE_CHUNKS_AT[k]:
                    if k:
                        chunk_lo(c)
                multiply(k)
            for m in range(1, H1 // P, 2):
                dve.wait_ge(h1_summed, m + 1)
                dve.wait_ge(bc_ready, 1)
                nc.vector.tensor_scalar(h1[:, m, :], ps[:, H1_BANK[m], :], bc[:, m:m + 1], 0.0,
                                        ALU.add, ALU.max).then_inc(h1_ready[m], 1)
            dve.wait_ge(mlp_loaded, 80)
            dve.wait_ge(h2_summed, 2)
            nc.vector.tensor_scalar(h2[:, 1, :], ps[:, H2_BANK[1], :], b2_sb[:, 1:2], 0.0,
                                    ALU.add, ALU.max).then_inc(h2_ready[1], 1)

        @block.tensor
        def _(pe):
            def look_up_couple(m):
                pe.wait_ge(lookup_loaded[m], 64 if m == 0 else 48)
                for f, c, row in lookup_blocks(m):
                    i = lookup_order.index((f, c, row))
                    pe.wait_ge(onehot_ready, i + 1)
                    half = f % 2 * D
                    nc.tensor.matmul(ps[half:half + D, COUPLE_BANK[m], :], tbl[:, f, c * D:(c + 1) * D],
                                     onehot[:, i % ONEHOT_SLOTS, :], start=(c == 0),
                                     stop=(c == LOOKUP_ROWS[f] // LOOKUP_PARTS - 1)).then_inc(onehot_used, 1)

            def transpose_couple(n):
                pe.wait_ge(gathered[n], 16 * 2 * BT)
                if n >= 1:
                    pe.wait_ge(q_hi_ready, n)
                for bt in range(BT):
                    last = nc.tensor.transpose(ps[:, TP, bt * P:(bt + 1) * P],
                                               emb[:, bt, 2 * n * D:2 * (n + 1) * D], ident[:, :])
                last.then_inc(transposed, 1)

            def contract(k):
                kind, m, n = STEPS[k]
                if kind == "group":
                    g = GROUP_STEP.index(k)
                    c = g // CHUNK_GROUPS
                    at = g % CHUNK_GROUPS * GROUP_COLS
                    weights = [r[:, c % R_SLOTS, at + jj * P:at + (jj + 1) * P] for jj in range(2)]
                    right = [q[:, n % Q_SLOTS, jj] for jj in range(2)]
                else:
                    c = DIAG
                    weights = [rdiag[:, x * P:(x + 1) * P] for x in (m, n)]
                    right = [q[:, x % Q_SLOTS, 1] for x in (m, n)]
                    wait_q_spread(pe, m)
                wait_chunk_spread(pe, c)
                wait_q_spread(pe, n)
                if k >= T_SLOTS:
                    pe.wait_ge(prod_ready, k - T_SLOTS + 1)
                for jj in range(2):
                    for part in range(2):
                        last = nc.tensor.matmul(t_tile(k)[:, jj, :], weights[jj], right[jj][:, part, :],
                                                start=(part == 0), stop=(part == 1))
                last.then_inc(t_ready, 1)

            def sum_pairs(b):
                pe.wait_ge(prod_ready, 2 * b + 2)
                at = b % FILL_BATCHES
                if b >= FILL_BATCHES and at == 0:
                    pe.wait_ge(pij_ready, b // FILL_BATCHES)
                for x in range(4):
                    k = 2 * b + x // 2
                    last = nc.tensor.matmul(ps[STRIP * x:STRIP * (x + 1), ACC, :],
                                            sel[:, STRIP - 2 - 2 * at:2 * STRIP - 2 - 2 * at],
                                            prod[:, k % PROD_SLOTS, x % 2, :],
                                            start=(at == 0), stop=(at == FILL_BATCHES - 1))
                last.then_inc(pairs_summed, 1)

            def fold_weights(f):
                for o in range(2):
                    last = nc.tensor.matmul(ps[:, f, :], w_sb[:, o, f * P:(f + 1) * P], w1_sb[:, o, :],
                                            start=(o == 0), stop=(o == 1))
                last.then_inc(wc_summed, 1)

            for m in range(LOOKED_UP):
                look_up_couple(m)
            pe.wait_ge(weights_loaded, 64)
            for m in range(H1 // P):
                for o in range(2):
                    last = nc.tensor.matmul(ps[:, 4, m:m + 1], w1_sb[:, o, m * P:(m + 1) * P], bp_sb[:, o:o + 1],
                                            start=(o == 0), stop=(o == 1))
            last.then_inc(bc_summed, 1)
            for f in range(FILLS):
                fold_weights(f)
            pe.wait_ge(ident_ready, 1)
            pe.wait_ge(sel_ready, 3)
            for k in range(N_STEPS):
                for n in COUPLES_AT[k]:
                    if n >= LOOKED_UP:
                        transpose_couple(n)
                if k < 2:
                    pe.wait_ge(wc_ready, 2 * k + 2)
                if k == 2:
                    pe.wait_ge(bc_ready, 1)
                contract(k)
                if k % 2 and k >= LAG:
                    sum_pairs((k - LAG) // 2)

            def h1_early(m):
                nc.tensor.matmul(ps[:, H1_BANK[m], :], w1d_sb[:, m * P:(m + 1) * P], dense_sb[:, :],
                                 start=True, stop=False)
                for f in range(FILLS - 1):
                    nc.tensor.matmul(ps[:, H1_BANK[m], :], wc[:, f, m * P:(m + 1) * P], pij[:, f, :],
                                     start=False, stop=False)

            pe.wait_ge(mlp_loaded, 80)
            pe.wait_ge(pij_ready, FILLS - 1)
            pe.wait_ge(prod_ready, N_STEPS - 2)
            for m in (0, 1):
                h1_early(m)
            sum_pairs(BATCHES - 1)
            for m in (2, 3):
                h1_early(m)
            pe.wait_ge(pij_ready, FILLS)
            for m in range(H1 // P):
                nc.tensor.matmul(ps[:, H1_BANK[m], :], wc[:, FILLS - 1, m * P:(m + 1) * P], pij[:, FILLS - 1, :],
                                 start=False, stop=True).then_inc(h1_summed, 1)
            for kk in range(H1 // P):
                pe.wait_ge(h1_ready[kk], 1)
                for m in range(H2 // P):
                    mm = nc.tensor.matmul(ps[:, H2_BANK[m], :], w2_sb[:, kk, m * P:(m + 1) * P], h1[:, kk, :],
                                          start=(kk == 0), stop=(kk == H1 // P - 1))
                    if kk == H1 // P - 1:
                        mm.then_inc(h2_summed, 1)
            for kk in range(H2 // P):
                pe.wait_ge(h2_ready[kk], 1)
                mm = nc.tensor.matmul(ps[0:1, TP, :], w3_sb[:, kk:kk + 1], h2[:, kk, :],
                                      start=(kk == 0), stop=(kk == H2 // P - 1))
            mm.then_inc(y_summed, 1)


def kernel(**inputs):
    import numpy as _np
    import concourse.bacc as _bacc
    from concourse import mybir as _mybir
    from concourse.bass_utils import run_bass_kernel_spmd as _run

    a = {name: _np.asarray(x) for name, x in inputs.items()}
    k = a["L0_rec_kernel"]
    group_part = k[:, _np.array(chunk_pairs()), :].reshape(D, GROUP_CHUNKS, 2, HALF_COLS)
    diag_part = _np.concatenate([k[:, _np.array(diag_pairs()), :], _np.zeros((D, COUPLES, D), k.dtype)], axis=2)
    k_chunks = _np.concatenate([group_part, diag_part.reshape(D, 1, 2, HALF_COLS)], axis=1)
    k_chunks = k_chunks.transpose(1, 2, 0, 3).reshape(GROUP_CHUNKS + 1, P, HALF_COLS)
    w = _np.concatenate([a["L0_rec_W"], _np.zeros((D1, 1), k.dtype)], axis=1)[:, _np.array(slot_pairs())]
    arrays = {
        "ids_t": a["ids"].T[:2 * LOOKED_UP],
        "row_numbers": lookup_rows(),
        "ids": a["ids"].reshape(BT, P, FIELDS).transpose(1, 2, 0),
        "k_chunks": k_chunks,
        "w_slots": w.reshape(2, P, FILLS * P).transpose(1, 0, 2),
        "b_pair": a["L0_rec_b"].reshape(2, P).T,
        "w1": a["W_top1"],
        "b1": a["b_top1"].reshape(H1 // P, P).T,
        "w2": a["W_top2"],
        "b2": a["b_top2"].reshape(H2 // P, P).T,
        "w3": a["W_top3"].reshape(H2 // P, P).T,
        "dense_t": a["dense_ctx"].T,
    }
    for f in range(FIELDS):
        arrays[f"tbl_{f}"] = a[f"tbl_{f}"]
    arrays = {f"in_{name}": _np.ascontiguousarray(x) for name, x in arrays.items()}

    nc = _bacc.Bacc("TRN2", target_bir_lowering=False, num_devices=1)
    dram = {name[3:]: nc.dram_tensor(name, x.shape, _mybir.dt.from_np(x.dtype), kind="ExternalInput").ap()
            for name, x in arrays.items()}
    out = nc.dram_tensor("out_0", (BATCH, 1), _mybir.dt.float32, kind="ExternalOutput").ap()
    tables = [dram.pop(f"tbl_{f}") for f in range(FIELDS)]
    build(nc, tables=tables, out=out, **dram)
    result = _run(nc, [arrays], core_ids=[0])
    return result.results[0]["out_0"]
```

```python
from contextlib import ExitStack

import numpy as np

import concourse.bass as bass
from concourse import mybir

F32 = mybir.dt.float32
F32R = mybir.dt.float32r
I32 = mybir.dt.int32
U32 = mybir.dt.uint32
ALU = mybir.AluOpType
ACT = mybir.ActivationFunctionType

P = 128
BATCH = 512
BT = BATCH // P
FIELDS = 32
D = 64
COUPLES = FIELDS // 2
PAIRS = FIELDS * (FIELDS - 1) // 2
D1 = 256
DENSE = 16
H1 = 512
H2 = 256
GROUPS = COUPLES * (COUPLES - 1) // 2
GROUP_COLS = 4 * D
CHUNK_GROUPS = 8
CHUNK_COLS = CHUNK_GROUPS * GROUP_COLS
HALF_COLS = CHUNK_COLS // 2
GROUP_CHUNKS = GROUPS // CHUNK_GROUPS
DIAG = GROUP_CHUNKS

ORDER = (0, 2, 3, 1) + tuple(range(4, COUPLES))
LOOKUP_PLACES = (0, 3)
LOOKED_UP = len(LOOKUP_PLACES)
LOOKUP_ROWS = (1000, 1000, 1000, 1250)
LOOKUP_PARTS = 125
LOOKUP_MAX = max(LOOKUP_ROWS) // LOOKUP_PARTS

WARM_UPS = 10

T_SLOTS = 3
PROD_SLOTS = 4
Q_SLOTS = 4
EXPANDED = Q_SLOTS
HEAD_STEPS = 3
S_SLOTS = 2
R_SLOTS = 3
ONEHOT_SLOTS = 8
RAW_SLOTS = 3
HI_SLOTS = 2
POOL_CHUNKS_FROM = 4
POOL_GATHERS_TWO_AT = 10
STRIP = 32
FILL_TILES = 64
FILLS = 4


def make_plan():
    steps, first = [], {}
    for n in range(COUPLES):
        first[n] = len(steps)
        if n % 2 and n > 1:
            steps.append(("diag", n - 1, n))
        steps += [("group", m, n) for m in range(n)]
        if n == 2:
            steps.append(("diag", 0, 1))
    group_step = [k for k, s in enumerate(steps) if s[0] == "group"]
    last_use = {}
    for k, (kind, m, n) in enumerate(steps):
        last_use[n] = k
        if kind == "diag":
            last_use[m] = k
    couples_at = {k: [] for k in range(len(steps))}
    lo_parts_at = {k: [] for k in range(len(steps))}
    for n in range(COUPLES):
        if n < EXPANDED:
            continue
        at = HEAD_STEPS if n == EXPANDED else first[n] - (5 if n < 7 else 6 if n < 8 else 8)
        couples_at[at].append(n)
        late = at + (1 if n > 7 else 0)
        lo_parts_at[late].append((n, 0))
        lo_parts_at[late + 1].append((n, 1))
    order = [0, DIAG] + list(range(1, GROUP_CHUNKS))
    chunks_at = {k: [] for k in range(len(steps))}
    late_chunks_at = {k: [] for k in range(len(steps))}
    for c in range(1, GROUP_CHUNKS):
        if c == 1:
            late_chunks_at[HEAD_STEPS + 1].append(c)
        else:
            at = group_step[c * CHUNK_GROUPS] - (11 if c < R_SLOTS else 14)
            chunks_at[at].append(c)
            late_chunks_at[at + 3].append(c)
    return steps, group_step, last_use, couples_at, lo_parts_at, chunks_at, late_chunks_at, order


(STEPS, GROUP_STEP, LAST_USE, COUPLES_AT, LO_PARTS_AT, CHUNKS_AT, LATE_CHUNKS_AT,
 CHUNK_ORDER) = make_plan()
N_STEPS = len(STEPS)
BATCHES = N_STEPS // 2
FILL_BATCHES = FILL_TILES // 4

SLOT_USES = [("double", 0, 0), ("double", 0, 1), ("double", 1, 0), ("double", 1, 1), ("step", 0),
             ("double", 2, 0), ("double", 2, 1), ("step", 1), ("step", 2), ("double", 3, 0), ("double", 3, 1)]
SLOT_USES += [("step", k) for k in range(HEAD_STEPS, N_STEPS)]
MLP_LOADS = 9
LOAD_STEP = N_STEPS // 2
DENSE_STEP = N_STEPS - 16
LAG = 3


def lookup_rows():
    part = np.arange(LOOKUP_PARTS)[:, None]
    return np.concatenate([part * (v // LOOKUP_PARTS) + np.arange(v // LOOKUP_PARTS)
                           for v in LOOKUP_ROWS], axis=1).astype(np.float32)


def fields_of(place):
    return 2 * ORDER[place], 2 * ORDER[place] + 1


def pair_index(i, j):
    i, j = min(i, j), max(i, j)
    return i * FIELDS - i * (i + 1) // 2 + j - i - 1


def chunk_pairs():
    return [(i, j) for kind, m, n in STEPS if kind == "group" for j in fields_of(n) for i in fields_of(m)]


def diag_pairs():
    return [pair_index(*fields_of(m)) for m in range(COUPLES)]


def slot_pairs():
    rows = [PAIRS] * (FILLS * P)
    for k, (kind, m, n) in enumerate(STEPS):
        for jj in range(2):
            tile = 2 * k + jj
            row = tile // FILL_TILES * P + STRIP * (tile % 4) + 2 * (tile % FILL_TILES // 4)
            if kind == "group":
                for half in range(2):
                    rows[row + half] = pair_index(fields_of(m)[half], fields_of(n)[jj])
            else:
                rows[row] = pair_index(*fields_of((m, n)[jj]))
    return rows


def build(nc, ids, ids_t, row_numbers, tables, k_chunks, w_t, b_pair, w1, w1_dense, b1, w2, b2, w3, dense_t, out):
    with ExitStack() as ctx:
        def sb(name, shape, dt=F32):
            return ctx.enter_context(nc.sbuf_tensor(name, shape, dt))

        def sem(name):
            return ctx.enter_context(nc.semaphore(name))

        ids_sb = sb("ids_sb", [P, FIELDS, BT], I32)
        emb = sb("emb", [P, BT, FIELDS * D])
        et = sb("et", [P, COUPLES, BATCH])
        split = sb("split", [P, S_SLOTS, 2, BATCH], F32R)
        q = sb("q", [P, Q_SLOTS, 2, 2, BATCH], F32R)
        raw = sb("raw", [P, RAW_SLOTS, HALF_COLS])
        khi = sb("khi", [P, HI_SLOTS, HALF_COLS], F32R)
        r = sb("r", [P, R_SLOTS, CHUNK_COLS], F32R)
        rdiag = sb("rdiag", [P, CHUNK_COLS], F32R)
        row_of = sb("row_of", [LOOKUP_PARTS, sum(LOOKUP_ROWS) // LOOKUP_PARTS])
        prod = sb("prod", [P, PROD_SLOTS, 2, BATCH])
        pij = sb("pij", [P, FILLS, BATCH])
        ident = sb("ident", [P, P])
        double = sb("double", [P, 2, 2, D], F32R)
        sel = sb("sel", [P, 2 * STRIP - 2])
        w_sb = sb("w_sb", [P, FILLS, D1])
        bp_sb = sb("bp_sb", [P, D1 // P])
        w1_sb = sb("w1_sb", [P, 2, H1])
        dense_raw = sb("dense_raw", [P, BATCH])
        dense_x = sb("dense_x", [P, BATCH], F32R)
        w1d_raw = sb("w1d_raw", [P, H1])
        dense_w = sb("dense_w", [P, H1], F32R)
        b1_sb = sb("b1_sb", [P, H1 // P])
        w2_sb = sb("w2_sb", [P, H1 // P, H2])
        b2_sb = sb("b2_sb", [P, H2 // P])
        w3_sb = sb("w3_sb", [P, H2 // P])
        y_sb = sb("y_sb", [1, BATCH])
        tbl = emb[0:LOOKUP_PARTS, :, (FIELDS - LOOKUP_MAX) * D:]
        onehot = et[0:LOOKUP_PARTS, COUPLES - ONEHOT_SLOTS:, :]
        ids_all = pij[0:LOOKUP_PARTS, :, :].bitcast(I32)

        h1 = emb[:, 0, :].rearrange("p (m b) -> p m b", b=BATCH)
        h2 = emb[:, 1, 0:2 * BATCH].rearrange("p (m b) -> p m b", b=BATCH)
        z = emb[:, 2, 0:2 * BATCH].rearrange("p (m b) -> p m b", b=BATCH)

        ps = ctx.enter_context(nc.psum_tensor("ps", [P, 8, BATCH], F32))

        def t_slot(*use):
            return SLOT_USES.index(use) % T_SLOTS

        def t_banks(*use):
            s = t_slot(*use)
            return ps[:, 2 * s:2 * s + 2, :]

        ACC, TP = 6, 7
        COUPLE_BANK = [5] + [ACC if n in LOOKUP_PLACES else TP for n in range(1, COUPLES)]
        z_slot, *h1_slots = [t_slot("step", k) for k in range(N_STEPS - 3, N_STEPS)]
        Z_BANK = (2 * z_slot, 2 * z_slot + 1)
        H1_BANK = [2 * x + half for x in h1_slots for half in range(2)]
        H2_BANK = (ACC, TP)
        Y_BANK = Z_BANK[0]

        ids_loaded = sem("ids_loaded")
        mlp_loaded = sem("mlp_loaded")
        gathered = [sem(f"gathered{c}") for c in range(COUPLES)]
        raw_loaded = [sem(f"raw_loaded{s}") for s in range(RAW_SLOTS)]
        r_spread = [sem(f"r_spread{s}") for s in range(R_SLOTS)]
        diag_spread = sem("diag_spread")
        q_spread = [sem(f"q_spread{s}") for s in range(Q_SLOTS)]
        lookup_ids_loaded = [sem(f"lookup_ids_loaded{m}") for m in range(LOOKED_UP)]
        row_of_loaded = sem("row_of_loaded")
        tables_loaded = [sem(f"tables_loaded{m}") for m in range(LOOKED_UP)]
        onehot_ready = sem("onehot_ready")
        onehot_used = sem("onehot_used")
        consts_zeroed = sem("consts_zeroed")
        ident_ready = sem("ident_ready")
        sel_ready = sem("sel_ready")
        transposed = sem("transposed")
        double_ready = sem("double_ready")
        doubled = sem("doubled")
        q_doubled = sem("q_doubled")
        q_hi_ready = sem("q_hi_ready")
        q_lo_ready = sem("q_lo_ready")
        k_hi_ready = sem("k_hi_ready")
        k_lo_ready = sem("k_lo_ready")
        k_lo_ready_pool = sem("k_lo_ready_pool")
        t_ready = sem("t_ready")
        prod_ready = sem("prod_ready")
        pairs_summed = sem("pairs_summed")
        pij_ready = sem("pij_ready")
        dense_hi_ready = sem("dense_hi_ready")
        dense_ready = sem("dense_ready")
        z_summed = sem("z_summed")
        z_ready = [sem(f"z_ready{m}") for m in range(D1 // P)]
        h1_summed = sem("h1_summed")
        h1_ready = [sem(f"h1_ready{m}") for m in range(H1 // P)]
        h2_summed = sem("h2_summed")
        h2_ready = [sem(f"h2_ready{m}") for m in range(H2 // P)]
        y_summed = sem("y_summed")
        y_ready = sem("y_ready")
        stored = sem("stored")

        place = {c: s for s, c in enumerate(CHUNK_ORDER)}

        def field_rows(field):
            return slice(field * D, (field + 1) * D)

        def couple_parts(n):
            return n + 1 + max(n + 1 - EXPANDED, 0)

        def made_by_pool(c):
            return POOL_CHUNKS_FROM <= c != DIAG

        def wait_chunk_spread(eng, c):
            if c == DIAG:
                eng.wait_ge(diag_spread, 64)
            else:
                eng.wait_ge(r_spread[c % R_SLOTS], 64 * (c // R_SLOTS + 1))

        def wait_q(eng, n):
            if n < EXPANDED:
                eng.wait_ge(q_doubled, 2 * (n + 1))
            else:
                eng.wait_ge(q_spread[n % Q_SLOTS], 32 * (n // Q_SLOTS))

        def lookup_blocks(m):
            blocks = [v // LOOKUP_PARTS for v in LOOKUP_ROWS]
            return [(f, c, sum(blocks[:f]) + c) for c in range(LOOKUP_MAX) for f in (2 * m, 2 * m + 1)
                    if c < blocks[f]]

        lookup_order = [x for m in range(LOOKED_UP) for x in lookup_blocks(m)]

        block = ctx.enter_context(nc.Block())

        @block.sync
        def _(sp):
            def load_chunk(s):
                if s >= RAW_SLOTS:
                    wait_chunk_spread(sp, CHUNK_ORDER[s - RAW_SLOTS])
                sp.dma_start(raw[:, s % RAW_SLOTS, :], k_chunks[CHUNK_ORDER[s]]).then_inc(
                    raw_loaded[s % RAW_SLOTS], 16)

            def load_lookup(m):
                sp.dma_start(ids_all[:, 2 * m:2 * m + 2, :],
                             ids_t[2 * m:2 * m + 2, :].unsqueeze(0).broadcast_to([LOOKUP_PARTS, 2, BATCH])
                             ).then_inc(lookup_ids_loaded[m], 16)
                for f in (2 * m, 2 * m + 1):
                    sp.dma_start(tbl[:, f, 0:LOOKUP_ROWS[f] // LOOKUP_PARTS * D],
                                 tables[f].rearrange("(p c) d -> p (c d)", p=LOOKUP_PARTS)
                                 ).then_inc(tables_loaded[m], 16)

            def spread_chunk(c):
                s = place[c]
                if made_by_pool(c):
                    sp.wait_ge(k_lo_ready_pool, c - POOL_CHUNKS_FROM + 1)
                else:
                    sp.wait_ge(k_lo_ready, s + 1)
                if c != DIAG and c >= R_SLOTS:
                    sp.wait_ge(t_ready, GROUP_STEP[(c - R_SLOTS + 1) * CHUNK_GROUPS - 1] + 1)
                dst = rdiag[:, :] if c == DIAG else r[:, c % R_SLOTS, :]
                done = diag_spread if c == DIAG else r_spread[c % R_SLOTS]
                for row, src in ((0, khi[:, s % HI_SLOTS, :].bitcast(F32)), (D, raw[:, s % RAW_SLOTS, :])):
                    for half in range(2):
                        sp.dma_start(dst[row:row + D, half * HALF_COLS:(half + 1) * HALF_COLS].bitcast(F32),
                                     src[half * D:(half + 1) * D, :]).then_inc(done, 16)

            def spread_field(n, field):
                sp.wait_ge(q_lo_ready, couple_parts(n) - 1 + field)
                own, other = field_rows(field), field_rows(1 - field)
                sp.dma_start(q[other, n % Q_SLOTS, field, :, :].bitcast(F32),
                             q[own, n % Q_SLOTS, field, :, :].bitcast(F32)).then_inc(q_spread[n % Q_SLOTS], 16)

            sp.dma_start(ids_sb[:, :, :], ids).then_inc(ids_loaded, 16)
            sp.dma_start(row_of[:, :], row_numbers).then_inc(row_of_loaded, 16)
            load_lookup(0)
            load_chunk(0)
            load_lookup(1)
            load_chunk(1)
            spread_chunk(CHUNK_ORDER[0])
            load_chunk(2)
            spread_chunk(CHUNK_ORDER[1])
            load_chunk(3)
            mlp_loads = [
                (w_sb[:, :, :], w_t), (w1_sb[:, :, :], w1[0:D1, :].rearrange("(o p) m -> p o m", p=P)),
                (w1d_raw[:, :], w1_dense), (dense_raw[:, :], dense_t),
                (w2_sb[:, :, :], w2.rearrange("(k p) m -> p k m", p=P)),
                (bp_sb[:, :], b_pair), (b1_sb[:, :], b1), (b2_sb[:, :], b2), (w3_sb[:, :], w3),
            ]
            for k in range(HEAD_STEPS, N_STEPS):
                for n, field in LO_PARTS_AT[k]:
                    spread_field(n, field)
                for c in LATE_CHUNKS_AT[k]:
                    spread_chunk(c)
                    s = place[c] - 1 + RAW_SLOTS
                    if s < len(CHUNK_ORDER):
                        load_chunk(s)
                load, rest = divmod(k - LOAD_STEP, 4)
                if rest == 0 and 0 <= load < len(mlp_loads):
                    sp.dma_start(*mlp_loads[load]).then_inc(mlp_loaded, 16)
            sp.wait_ge(y_ready, 1)
            sp.dma_start(out.rearrange("b o -> o b"), y_sb[:, :]).then_inc(stored, 16)
            sp.wait_ge(stored, 16)

        @block.gpsimd
        def _(pool):
            nc.gpsimd.memset(ident[:, :], 0.0).then_inc(consts_zeroed, 1)
            pool.wait_ge(consts_zeroed, 1)
            nc.gpsimd.affine_select(out=ident[:, :], in_=ident[:, :], compare_op=ALU.not_equal, fill=1.0,
                                    base=0, pattern=[[-1, P]], channel_multiplier=1).then_inc(ident_ready, 1)
            pool.wait_ge(ids_loaded, 16)

            def gather_couple(c):
                if 2 * (c + 1) > FIELDS - LOOKUP_MAX:
                    pool.wait_ge(onehot_used, len(lookup_order))
                for f in (2 * c, 2 * c + 1):
                    for bt in range(BT):
                        pool.indirect_dma_start(
                            emb[:, bt, f * D:(f + 1) * D], None, tables[f],
                            bass.IndirectOffsetOnAxis(ids_sb[:, f, bt:bt + 1].bitcast(U32), 0),
                        ).then_inc(gathered[c], 16)

            def chunk_lo(c):
                s = place[c]
                pool.wait_ge(k_hi_ready, s + 1)
                nc.gpsimd.tensor_tensor(raw[:, s % RAW_SLOTS, :], raw[:, s % RAW_SLOTS, :],
                                        khi[:, s % HI_SLOTS, :].bitcast(F32),
                                        ALU.subtract).then_inc(k_lo_ready_pool, 1)

            chunk = POOL_CHUNKS_FROM
            for c in range(LOOKED_UP, COUPLES):
                gather_couple(c)
                if c >= COUPLES // 2 and c != POOL_GATHERS_TWO_AT:
                    chunk_lo(chunk)
                    chunk += 1
            for c in range(chunk, GROUP_CHUNKS):
                chunk_lo(c)

        @block.scalar
        def _(act):
            def chunk_hi(c):
                s = place[c]
                act.wait_ge(raw_loaded[s % RAW_SLOTS], 16 * (s // RAW_SLOTS + 1))
                if s >= HI_SLOTS:
                    wait_chunk_spread(act, CHUNK_ORDER[s - HI_SLOTS])
                nc.scalar.activation(khi[:, s % HI_SLOTS, :], raw[:, s % RAW_SLOTS, :],
                                     ACT.Copy).then_inc(k_hi_ready, 1)

            def couple_hi(n):
                looked_up = sum(x <= n for x in LOOKUP_PLACES)
                if n in LOOKUP_PLACES:
                    act.wait_ge(onehot_used, sum(len(lookup_blocks(m)) for m in range(looked_up)))
                else:
                    act.wait_ge(transposed, n + 1 - looked_up)
                nc.scalar.activation(et[:, n, :], ps[:, COUPLE_BANK[n], :], ACT.Copy)
                if n < EXPANDED:
                    if n >= S_SLOTS:
                        wait_q(act, n - S_SLOTS)
                    nc.scalar.activation(split[:, n % S_SLOTS, 0, :], ps[:, COUPLE_BANK[n], :],
                                         ACT.Copy).then_inc(q_hi_ready, 1)
                else:
                    act.wait_ge(t_ready, LAST_USE[n - Q_SLOTS] + 1)
                    for field in range(2):
                        own = field_rows(field)
                        nc.scalar.activation(q[own, n % Q_SLOTS, field, 0, :], ps[own, COUPLE_BANK[n], :],
                                             ACT.Copy).then_inc(q_hi_ready, 1)

            def take_doubled(n):
                for field in range(2):
                    act.wait_ge(doubled, 2 * n + field + 1)
                    nc.scalar.activation(q[:, n % Q_SLOTS, field, :, :], t_banks("double", n, field),
                                         ACT.Copy).then_inc(q_doubled, 1)

            def take_pairs(f):
                act.wait_ge(pairs_summed, FILL_BATCHES * (f + 1))
                nc.scalar.activation(pij[:, f, :], ps[:, ACC, :], ACT.Copy).then_inc(pij_ready, 1)

            act.wait_ge(ident_ready, 1)
            for field in range(2):
                nc.scalar.activation(double[:, field, :, :],
                                     ident[:, field * D:(field + 1) * D].unsqueeze(1).broadcast_to([P, 2, D]),
                                     ACT.Copy).then_inc(double_ready, 1)
            chunk_hi(CHUNK_ORDER[0])
            couple_hi(0)
            couple_hi(1)
            take_doubled(0)
            take_doubled(1)
            couple_hi(2)
            chunk_hi(CHUNK_ORDER[1])
            take_doubled(2)
            couple_hi(3)
            take_doubled(3)
            chunk_hi(CHUNK_ORDER[2])
            for k in range(HEAD_STEPS, N_STEPS):
                for n in COUPLES_AT[k]:
                    couple_hi(n)
                for c in CHUNKS_AT[k]:
                    chunk_hi(c)
                if k == DENSE_STEP:
                    act.wait_ge(mlp_loaded, 16 * MLP_LOADS)
                    nc.scalar.activation(dense_x[:, :], dense_raw[:, :], ACT.Copy).then_inc(dense_hi_ready, 1)
                    nc.scalar.activation(dense_w[:, :], w1d_raw[:, :], ACT.Copy).then_inc(dense_hi_ready, 1)
                b = (k - LAG) // 2
                if k % 2 and k > LAG and (b + 1) % FILL_BATCHES == 0:
                    take_pairs(b // FILL_BATCHES)
            take_pairs(FILLS - 1)
            act.wait_ge(mlp_loaded, 16 * MLP_LOADS)
            act.wait_ge(z_summed, 1)
            nc.scalar.activation(z[:, 0, :], ps[:, Z_BANK[0], :], ACT.Identity,
                                 bias=bp_sb[:, 0:1]).then_inc(z_ready[0], 1)
            for m in range(0, H1 // P, 2):
                act.wait_ge(h1_summed, m + 1)
                nc.scalar.activation(h1[:, m, :], ps[:, H1_BANK[m], :], ACT.Relu,
                                     bias=b1_sb[:, m:m + 1]).then_inc(h1_ready[m], 1)
            act.wait_ge(h2_summed, 1)
            nc.scalar.activation(h2[:, 0, :], ps[:, H2_BANK[0], :], ACT.Relu,
                                 bias=b2_sb[:, 0:1]).then_inc(h2_ready[0], 1)
            act.wait_ge(y_summed, 1)
            nc.scalar.activation(y_sb[:, :], ps[0:1, Y_BANK, :], ACT.Copy).then_inc(y_ready, 1)

        @block.vector
        def _(dve):
            def chunk_lo(c):
                s = place[c]
                dve.wait_ge(k_hi_ready, s + 1)
                nc.vector.tensor_tensor(raw[:, s % RAW_SLOTS, :], raw[:, s % RAW_SLOTS, :],
                                        khi[:, s % HI_SLOTS, :].bitcast(F32),
                                        ALU.subtract).then_inc(k_lo_ready, 1)

            def couple_lo(n):
                dve.wait_ge(q_hi_ready, couple_parts(n))
                nc.vector.tensor_tensor(split[:, n % S_SLOTS, 1, :], et[:, n, :],
                                        split[:, n % S_SLOTS, 0, :].bitcast(F32),
                                        ALU.subtract).then_inc(q_lo_ready, 1)

            def field_lo(n, field):
                own = field_rows(field)
                dve.wait_ge(q_hi_ready, couple_parts(n) - 1 + field)
                nc.vector.tensor_tensor(q[own, n % Q_SLOTS, field, 1, :], et[own, n, :],
                                        q[own, n % Q_SLOTS, field, 0, :].bitcast(F32),
                                        ALU.subtract).then_inc(q_lo_ready, 1)

            def multiply(k):
                kind, m, n = STEPS[k]
                dve.wait_ge(t_ready, k + 1)
                if k >= PROD_SLOTS:
                    dve.wait_ge(pairs_summed, (k - PROD_SLOTS) // 2 + 1)
                p_i = et[:, m, :].unsqueeze(1).broadcast_to([P, 2, BATCH]) if kind == "group" else et[:, m:n + 1, :]
                nc.vector.tensor_tensor(prod[:, k % PROD_SLOTS, :, :], t_banks("step", k), p_i,
                                        ALU.mult).then_inc(prod_ready, 1)

            def make_onehots(start, end):
                for i in range(start, end):
                    f, c, row = lookup_order[i]
                    if i >= ONEHOT_SLOTS:
                        dve.wait_ge(onehot_used, i - ONEHOT_SLOTS + 1)
                    dve.wait_ge(row_of_loaded, 16)
                    dve.wait_ge(lookup_ids_loaded[f // 2], 16)
                    nc.vector.tensor_scalar(onehot[:, i % ONEHOT_SLOTS, :], ids_all[:, f, :],
                                            row_of[:, row:row + 1], None, ALU.is_equal).then_inc(onehot_ready, 1)

            nc.vector.memset(sel[:, :], 0.0).then_inc(sel_ready, 1)
            dve.wait_ge(sel_ready, 1)
            nc.vector.memset(sel[0:D, STRIP - 2:STRIP - 1], 1.0).then_inc(sel_ready, 1)
            nc.vector.memset(sel[D:P, STRIP - 1:STRIP], 1.0).then_inc(sel_ready, 1)
            first_lookups = len(lookup_blocks(0))
            make_onehots(0, first_lookups)
            chunk_lo(CHUNK_ORDER[0])
            make_onehots(first_lookups, first_lookups + 4)
            couple_lo(0)
            make_onehots(first_lookups + 4, first_lookups + 8)
            couple_lo(1)
            make_onehots(first_lookups + 8, len(lookup_order))
            couple_lo(2)
            chunk_lo(CHUNK_ORDER[1])
            multiply(0)
            couple_lo(3)
            dense_lo_parts = ((dense_x, dense_raw, P // 2, P), (dense_w, w1d_raw, P // 4, P // 2),
                              (dense_w, w1d_raw, 3 * P // 4, P))
            for k in range(1, N_STEPS):
                if k >= HEAD_STEPS:
                    for n, field in LO_PARTS_AT[k]:
                        field_lo(n, field)
                    for c in LATE_CHUNKS_AT[k]:
                        if not made_by_pool(c):
                            chunk_lo(c)
                if DENSE_STEP < k <= DENSE_STEP + len(dense_lo_parts):
                    part, whole, lo, hi = dense_lo_parts[k - DENSE_STEP - 1]
                    dve.wait_ge(dense_hi_ready, 2)
                    nc.vector.tensor_tensor(part[lo:hi, :], whole[lo:hi, :], part[lo:hi, :].bitcast(F32),
                                            ALU.subtract).then_inc(dense_ready, 1)
                multiply(k)
            dve.wait_ge(mlp_loaded, 16 * MLP_LOADS)
            dve.wait_ge(z_summed, 2)
            nc.vector.tensor_scalar(z[:, 1, :], ps[:, Z_BANK[1], :], bp_sb[:, 1:2], None,
                                    ALU.add).then_inc(z_ready[1], 1)
            for m in range(1, H1 // P, 2):
                dve.wait_ge(h1_summed, m + 1)
                nc.vector.tensor_scalar(h1[:, m, :], ps[:, H1_BANK[m], :], b1_sb[:, m:m + 1], 0.0,
                                        ALU.add, ALU.max).then_inc(h1_ready[m], 1)
            dve.wait_ge(h2_summed, 2)
            nc.vector.tensor_scalar(h2[:, 1, :], ps[:, H2_BANK[1], :], b2_sb[:, 1:2], 0.0,
                                    ALU.add, ALU.max).then_inc(h2_ready[1], 1)

        @block.tensor
        def _(pe):
            def look_up(start, end):
                for i in range(start, end):
                    f, c, row = lookup_order[i]
                    m = f // 2
                    pe.wait_ge(tables_loaded[m], 32)
                    pe.wait_ge(onehot_ready, i + 1)
                    half = f % 2 * D
                    nc.tensor.matmul(ps[half:half + D, COUPLE_BANK[LOOKUP_PLACES[m]], :], tbl[:, f, c * D:(c + 1) * D],
                                     onehot[:, i % ONEHOT_SLOTS, :], start=(c == 0),
                                     stop=(c == LOOKUP_ROWS[f] // LOOKUP_PARTS - 1)).then_inc(onehot_used, 1)

            def transpose_couple(n):
                c = ORDER[n]
                pe.wait_ge(gathered[c], 16 * 2 * BT)
                before = [x for x in range(n) if x not in LOOKUP_PLACES]
                if before:
                    pe.wait_ge(q_hi_ready, couple_parts(before[-1]))
                for bt in range(BT):
                    last = nc.tensor.transpose(ps[:, TP, bt * P:(bt + 1) * P],
                                               emb[:, bt, 2 * c * D:2 * (c + 1) * D], ident[:, :])
                last.then_inc(transposed, 1)

            def wait_slot(*use):
                u = SLOT_USES.index(use)
                if u >= T_SLOTS:
                    before = SLOT_USES[u - T_SLOTS]
                    if before[0] == "step":
                        pe.wait_ge(prod_ready, before[1] + 1)
                    else:
                        pe.wait_ge(q_doubled, 2 * before[1] + before[2] + 1)

            def double_couple(n):
                pe.wait_ge(double_ready, 2)
                pe.wait_ge(q_lo_ready, n + 1)
                for field in range(2):
                    wait_slot("double", n, field)
                    for part in range(2):
                        last = nc.tensor.matmul(t_banks("double", n, field)[:, part, :], double[:, field, :, :],
                                                split[:, n % S_SLOTS, part, :], start=True, stop=True)
                    last.then_inc(doubled, 1)

            def contract(k):
                kind, m, n = STEPS[k]
                if kind == "group":
                    g = GROUP_STEP.index(k)
                    c = g // CHUNK_GROUPS
                    at = g % CHUNK_GROUPS * GROUP_COLS
                    weights = [r[:, c % R_SLOTS, at + jj * P:at + (jj + 1) * P] for jj in range(2)]
                    right = [q[:, n % Q_SLOTS, jj] for jj in range(2)]
                else:
                    c = DIAG
                    weights = [rdiag[:, x * P:(x + 1) * P] for x in (m, n)]
                    right = [q[:, x % Q_SLOTS, 1] for x in (m, n)]
                    wait_q(pe, m)
                wait_chunk_spread(pe, c)
                wait_q(pe, n)
                wait_slot("step", k)
                for jj in range(2):
                    for part in range(2):
                        last = nc.tensor.matmul(t_banks("step", k)[:, jj, :], weights[jj], right[jj][:, part, :],
                                                start=(part == 0), stop=(part == 1))
                last.then_inc(t_ready, 1)

            def sum_pairs(b):
                pe.wait_ge(prod_ready, 2 * b + 2)
                at = b % FILL_BATCHES
                if b == 0:
                    pe.wait_ge(q_hi_ready, LOOKUP_PLACES[1] + 1)
                if b >= FILL_BATCHES and at == 0:
                    pe.wait_ge(pij_ready, b // FILL_BATCHES)
                for x in range(4):
                    k = 2 * b + x // 2
                    last = nc.tensor.matmul(ps[STRIP * x:STRIP * (x + 1), ACC, :],
                                            sel[:, STRIP - 2 - 2 * at:2 * STRIP - 2 - 2 * at],
                                            prod[:, k % PROD_SLOTS, x % 2, :],
                                            start=(at == 0), stop=(at == FILL_BATCHES - 1))
                last.then_inc(pairs_summed, 1)

            pe.wait_ge(ident_ready, 1)
            for _ in range(WARM_UPS):
                nc.tensor.matmul(ps[:, TP, 0:P], ident[:, :], ident[:, :], start=True, stop=True)
            first_lookups = len(lookup_blocks(0))
            look_up(0, first_lookups)
            transpose_couple(1)
            def look_up_second(start, end):
                look_up(first_lookups + start, first_lookups + end)

            look_up_second(0, 4)
            double_couple(0)
            look_up_second(4, 8)
            double_couple(1)
            look_up_second(8, 12)
            transpose_couple(2)
            contract(0)
            look_up_second(12, 14)
            double_couple(2)
            look_up_second(14, len(lookup_order) - first_lookups)
            contract(1)
            contract(2)
            double_couple(3)
            pe.wait_ge(sel_ready, 3)
            for k in range(HEAD_STEPS, N_STEPS):
                for n in COUPLES_AT[k]:
                    transpose_couple(n)
                contract(k)
                if k % 2 and k >= LAG:
                    sum_pairs((k - LAG) // 2)

            def z_part(m, f):
                return nc.tensor.matmul(ps[:, Z_BANK[m], :], w_sb[:, f, m * P:(m + 1) * P], pij[:, f, :],
                                        start=(f == 0), stop=(f == FILLS - 1))

            pe.wait_ge(mlp_loaded, 16 * MLP_LOADS)
            pe.wait_ge(pij_ready, FILLS - 1)
            pe.wait_ge(prod_ready, N_STEPS - 2)
            for m in range(D1 // P):
                for f in range(FILLS - 1):
                    z_part(m, f)
            sum_pairs(BATCHES - 1)
            pe.wait_ge(dense_ready, 3)
            for m in range(H1 // P):
                nc.tensor.matmul(ps[:, H1_BANK[m], :], dense_w[:, m * P:(m + 1) * P], dense_x[:, :],
                                 start=True, stop=False)
            pe.wait_ge(pij_ready, FILLS)
            for m in range(D1 // P):
                z_part(m, FILLS - 1).then_inc(z_summed, 1)
            for kk in range(D1 // P):
                pe.wait_ge(z_ready[kk], 1)
                for m in range(H1 // P):
                    mm = nc.tensor.matmul(ps[:, H1_BANK[m], :], w1_sb[:, kk, m * P:(m + 1) * P], z[:, kk, :],
                                          start=False, stop=(kk == D1 // P - 1))
                    if kk == D1 // P - 1:
                        mm.then_inc(h1_summed, 1)
            for kk in range(H1 // P):
                pe.wait_ge(h1_ready[kk], 1)
                for m in range(H2 // P):
                    mm = nc.tensor.matmul(ps[:, H2_BANK[m], :], w2_sb[:, kk, m * P:(m + 1) * P], h1[:, kk, :],
                                          start=(kk == 0), stop=(kk == H1 // P - 1))
                    if kk == H1 // P - 1:
                        mm.then_inc(h2_summed, 1)
            for kk in range(H2 // P):
                pe.wait_ge(h2_ready[kk], 1)
                mm = nc.tensor.matmul(ps[0:1, Y_BANK, :], w3_sb[:, kk:kk + 1], h2[:, kk, :],
                                      start=(kk == 0), stop=(kk == H2 // P - 1))
            mm.then_inc(y_summed, 1)


def kernel(**inputs):
    import numpy as _np
    import concourse.bacc as _bacc
    from concourse import mybir as _mybir
    from concourse.bass_utils import run_bass_kernel_spmd as _run

    a = {name: _np.asarray(x) for name, x in inputs.items()}
    k = a["L0_rec_kernel"]
    pairs = chunk_pairs()
    blocks = [k[:, pair_index(i, j), :] if i < j else k[:, pair_index(i, j), :].T for i, j in pairs]
    group_part = _np.stack(blocks, axis=1).reshape(D, GROUP_CHUNKS, 2, HALF_COLS)
    diag_part = _np.concatenate([k[:, _np.array(diag_pairs()), :], _np.zeros((D, COUPLES, D), k.dtype)], axis=2)
    k_chunks = _np.concatenate([group_part, diag_part.reshape(D, 1, 2, HALF_COLS)], axis=1)
    k_chunks = k_chunks.transpose(1, 2, 0, 3).reshape(GROUP_CHUNKS + 1, P, HALF_COLS)
    w = _np.concatenate([a["L0_rec_W"], _np.zeros((D1, 1), k.dtype)], axis=1)[:, _np.array(slot_pairs())]

    def blocks_of_32(x):
        return _np.tile(_np.concatenate([x, _np.zeros_like(x)]), (P // (2 * DENSE), 1))

    arrays = {
        "ids_t": a["ids"].T[:2 * LOOKED_UP],
        "row_numbers": lookup_rows(),
        "ids": a["ids"].reshape(BT, P, FIELDS).transpose(1, 2, 0),
        "k_chunks": k_chunks,
        "w_t": w.T.reshape(FILLS, P, D1).transpose(1, 0, 2),
        "b_pair": a["L0_rec_b"].reshape(D1 // P, P).T,
        "w1": a["W_top1"],
        "b1": a["b_top1"].reshape(H1 // P, P).T,
        "w2": a["W_top2"],
        "b2": a["b_top2"].reshape(H2 // P, P).T,
        "w3": a["W_top3"].reshape(H2 // P, P).T,
        "dense_t": blocks_of_32(a["dense_ctx"].T),
        "w1_dense": blocks_of_32(a["W_top1"][D1:]),
    }
    for f in range(FIELDS):
        arrays[f"tbl_{f}"] = a[f"tbl_{f}"]
    arrays = {f"in_{name}": _np.ascontiguousarray(x) for name, x in arrays.items()}

    nc = _bacc.Bacc("TRN2", target_bir_lowering=False, num_devices=1)
    dram = {name[3:]: nc.dram_tensor(name, x.shape, _mybir.dt.from_np(x.dtype), kind="ExternalInput").ap()
            for name, x in arrays.items()}
    out = nc.dram_tensor("out_0", (BATCH, 1), _mybir.dt.float32, kind="ExternalOutput").ap()
    tables = [dram.pop(f"tbl_{f}") for f in range(FIELDS)]
    build(nc, tables=tables, out=out, **dram)
    result = _run(nc, [arrays], core_ids=[0])
    return result.results[0]["out_0"]
```
